# Optimizing a Trainium2 kernel written in Bass

```python
import numpy as np
import jax
import jax.numpy as jnp

def _softmax(x, axis=-1):
    return jax.nn.softmax(x, axis=axis)

def _gelu(x):
    return jax.nn.gelu(x, approximate=True)

def _silu(x):
    return jax.nn.silu(x)

def _sigmoid(x):
    return jax.nn.sigmoid(x)

def _layernorm(x, axis=-1, eps=1e-05):
    m = jnp.mean(x, axis=axis, keepdims=True)
    v = jnp.var(x, axis=axis, keepdims=True)
    return (x - m) / jnp.sqrt(v + eps)

def _scatter_add(tgt, idx, src, axis=0):
    return tgt.at[idx].add(src)

def _segment_sum(src, seg, n):
    return jax.ops.segment_sum(src, seg, n)
kernel_name = 'mk_sandwich_d1_jaxref_r4_2120cc'

def setup_inputs(seed: int=0):
    np.random.seed(seed)
    _w = jnp.asarray

    def _L0_attn_setup():
        import jax, jax.numpy as jnp
        import numpy as np
        DIM = 512
        HIDDEN = 1024
        BATCH = 4
        SEQ = 512
        key = jax.random.key(seed)
        ks = jax.random.split(key, 4)
        scale_in = 1.0 / np.sqrt(DIM)
        scale_out = 1.0 / np.sqrt(HIDDEN)
        return {'x': jax.random.normal(ks[0], (BATCH, SEQ, DIM), dtype=jnp.float32), 'W_in': jax.random.normal(ks[1], (HIDDEN, DIM), dtype=jnp.float32) * scale_in, 'b_in': jnp.zeros((HIDDEN,), dtype=jnp.float32), 'W_out': jax.random.normal(ks[2], (DIM, HIDDEN), dtype=jnp.float32) * scale_out, 'b_out': jnp.zeros((DIM,), dtype=jnp.float32), 'gamma': jnp.ones((HIDDEN,), dtype=jnp.float32), 'beta': jnp.zeros((HIDDEN,), dtype=jnp.float32)}
    _L0_attn_in = _L0_attn_setup()

    def _L0_ffn_setup():
        import jax, jax.numpy as jnp
        import numpy as np
        B, S, H, I = (1, 64, 512, 1536)

        def _quantized_matmul(x, w, scale):
            wq = w.astype(jnp.float8_e4m3fn).astype(x.dtype)
            y = jnp.einsum('bsi,io->bso', x, wq)
            return y * scale
        key = jax.random.key(seed)
        ks = jax.random.split(key, 7)
        return {'x': jax.random.normal(ks[0], (B, S, H), dtype=jnp.float32), 'gate_w': jax.random.normal(ks[1], (H, I), dtype=jnp.float32) * 0.02, 'up_w': jax.random.normal(ks[2], (H, I), dtype=jnp.float32) * 0.02, 'down_w': jax.random.normal(ks[3], (I, H), dtype=jnp.float32) * 0.02, 'gate_scale': jax.random.uniform(ks[4], (I,), dtype=jnp.float32, minval=0.5, maxval=1.5), 'up_scale': jax.random.uniform(ks[5], (I,), dtype=jnp.float32, minval=0.5, maxval=1.5), 'down_scale': jax.random.uniform(ks[6], (H,), dtype=jnp.float32, minval=0.5, maxval=1.5)}
    _L0_ffn_in = _L0_ffn_setup()
    _d = {'L0_attn_x': _L0_attn_in['x'], 'L0_attn_W_in': _L0_attn_in['W_in'], 'L0_attn_b_in': _L0_attn_in['b_in'], 'L0_attn_W_out': _L0_attn_in['W_out'], 'L0_attn_b_out': _L0_attn_in['b_out'], 'L0_attn_gamma': _L0_attn_in['gamma'], 'L0_attn_beta': _L0_attn_in['beta'], 'L0_ffn_gate_w': _L0_ffn_in['gate_w'], 'L0_ffn_up_w': _L0_ffn_in['up_w'], 'L0_ffn_down_w': _L0_ffn_in['down_w'], 'L0_ffn_gate_scale': _L0_ffn_in['gate_scale'], 'L0_ffn_up_scale': _L0_ffn_in['up_scale'], 'L0_ffn_down_scale': _L0_ffn_in['down_scale']}
    _x0 = _d['L0_attn_x']
    _d['L0_attn_x'] = jax.random.normal(jax.random.fold_in(jax.random.key(seed), 1), (2, 1024, 512), dtype=_x0.dtype)
    del _x0
    return _d

def reference(L0_attn_x, L0_attn_W_in, L0_attn_b_in, L0_attn_W_out, L0_attn_b_out, L0_attn_gamma, L0_attn_beta, L0_ffn_gate_w, L0_ffn_up_w, L0_ffn_down_w, L0_ffn_gate_scale, L0_ffn_up_scale, L0_ffn_down_scale):

    def _L0_attn_ref(x, W_in, b_in, W_out, b_out, gamma, beta):
        import jax, jax.numpy as jnp
        import numpy as np
        DIM = 512
        HIDDEN = 1024
        BATCH = 4
        SEQ = 512
        u = jnp.einsum('bsd,hd->bsh', x, W_in) + b_in

        def step(state, u_t):
            s = jnp.tanh(u_t + state * gamma + beta)
            return (s, s)
        init = jnp.zeros((x.shape[0], W_in.shape[0]), dtype=x.dtype)
        _, states = jax.lax.scan(step, init, jnp.swapaxes(u, 0, 1))
        states = jnp.swapaxes(states, 0, 1)
        y = jnp.einsum('bsh,dh->bsd', states, W_out) + b_out
        return y

    def _L0_ffn_ref(x, gate_w, up_w, down_w, gate_scale, up_scale, down_scale):
        import jax, jax.numpy as jnp
        import numpy as np
        B, S, H, I = (1, 64, 512, 1536)

        def _quantized_matmul(x, w, scale):
            wq = w.astype(jnp.float8_e4m3fn).astype(x.dtype)
            y = jnp.einsum('bsi,io->bso', x, wq)
            return y * scale
        gate = jax.nn.silu(_quantized_matmul(x, gate_w, gate_scale))
        up = _quantized_matmul(x, up_w, up_scale)
        fuse = gate * up
        return _quantized_matmul(fuse, down_w, down_scale)
    x = L0_attn_x
    x = x + _layernorm(_L0_attn_ref(_layernorm(x, axis=-1), L0_attn_W_in, L0_attn_b_in, L0_attn_W_out, L0_attn_b_out, L0_attn_gamma, L0_attn_beta), axis=-1)
    x = x + _layernorm(_L0_ffn_ref(_layernorm(x, axis=-1), L0_ffn_gate_w, L0_ffn_up_w, L0_ffn_down_w, L0_ffn_gate_scale, L0_ffn_up_scale, L0_ffn_down_scale), axis=-1)
    return x

_drawn_inputs = setup_inputs


def setup_inputs(seed=0):
    import zlib

    import numpy as np

    out = dict(_drawn_inputs(seed))
    spreads = {'L0_attn_b_in': (0.0, 0.1),
     'L0_attn_b_out': (0.0, 0.1),
     'L0_attn_gamma': (1.0, 0.2),
     'L0_attn_beta': (0.0, 0.1)}
    factors = {}
    for name, (base, spread) in spreads.items():
        noise = np.random.default_rng([zlib.crc32(name.encode()), seed]).standard_normal(out[name].shape)
        drawn = base * np.exp(spread * noise) if base else spread * noise
        out[name] = jnp.asarray(drawn.astype(out[name].dtype))
    for name, factor in factors.items():
        out[name] = (out[name] * factor).astype(out[name].dtype)
    return out
```

```python
from contextlib import ExitStack

import concourse.bass as bass
from concourse import mybir

P = 128
F32 = mybir.dt.float32
F32R = mybir.dt.float32r
I32 = mybir.dt.int32
ALU = mybir.AluOpType
ACT = mybir.ActivationFunctionType
AX_X = mybir.AxisListType.X
LN_EPS = 1e-5

EXPONENT_BITS = 0x7F800000
LEAST_NORMAL = 2.0 ** -6
ROUNDING_CONSTANT = 1.5 * 2.0 ** 20
E4M3FN_OVERFLOW = 464.0
HUGE = 1e38


class Queue:

    def __init__(self):
        self.items = {"sync": [], "tensor": [], "vector": [], "scalar": [], "gpsimd": []}
        self.added = 0

    def add(self, engine, slot, emit, rank=1):
        self.added += 1
        self.items[engine].append((slot, rank, self.added, emit))

    def emit(self, engine, eng, n):
        for _, _, _, emit in sorted(self.items[engine], key=lambda item: item[:3]):
            emit(eng, n)


def take(eng, sem, count=1):
    eng.wait_ge(sem, count)
    eng.sem_inc(sem, -count)


def pass_on(eng, sem):
    eng.sem_inc(sem, 1)


def recurrent_sandwich_kernel(nc, x, w_in_t, w_out_t, b_in, beta, gamma, b_out, gate_w, up_w, down_w,
                              gate_scale, up_scale, down_scale, identity, out):
    batch, seq, dim = x.shape
    hidden = w_in_t.shape[1]
    inner = gate_w.shape[1]
    KD = dim // P
    KH = hidden // P
    KI = inner // P
    T = 128
    NB = seq // T
    CH = KH * batch
    TOK = batch * T
    SLICES = 4
    TS = T // SLICES
    HALF = dim // 2
    assert T == P and TOK == 256 and dim == 512 and seq % T == 0

    x_blocks = x.rearrange("b (n t) d -> n t b d", t=T)
    out_blocks = out.rearrange("b (n t) d -> n t b d", t=T)

    with ExitStack() as ctx:
        def sb(name, shape, dt=F32):
            return ctx.enter_context(nc.sbuf_tensor(name, shape, dt))

        def ps(name, shape):
            return ctx.enter_context(nc.psum_tensor(name, shape, F32))

        def sem(name):
            return ctx.enter_context(nc.semaphore(name))

        w_in_sb = sb("w_in_sb", [P, KD, hidden])
        w_out_sb = sb("w_out_sb", [P, KH, dim])
        gate_q = sb("gate_q", [P, KD, inner], F32R)
        up_q = sb("up_q", [P, KD, inner], F32R)
        down_q = sb("down_q", [P, KI, dim], F32R)
        ident = sb("ident", [P, P])
        b_out_rows = sb("b_out_rows", [P, dim])
        down_scale_rows = sb("down_scale_rows", [P, dim])
        cols = sb("cols", [P, 3, KH])
        u_bias = sb("u_bias", [P, KH])
        gate_scale_raw = sb("gate_scale_raw", [P, KI])
        gate_scale_sb = sb("gate_scale_sb", [P, KI])
        up_scale_sb = sb("up_scale_sb", [P, KI])
        minus_half = sb("minus_half", [P, 2])
        warm = sb("warm", [P, 2])
        factors = sb("factors", [P, CH, 2])

        RAW = 3
        raw = sb("raw", [P, RAW, dim])
        rounder = sb("rounder", [P, RAW, dim])
        pieces = []
        for k in range(KD):
            for w_dram, w_q in ((gate_w, gate_q), (up_w, up_q)):
                for c in range(inner // dim):
                    pieces.append((w_dram[k * P:(k + 1) * P, c * dim:(c + 1) * dim],
                                   w_q[:, k, c * dim:(c + 1) * dim]))
        for i in range(KI):
            pieces.append((down_w[i * P:(i + 1) * P, :], down_q[:, i, :]))
        NP = len(pieces)
        peaks = sb("peaks", [P, NP])
        guard = sb("guard", [P, 4])

        x_in = sb("x_in", [P, batch, dim])
        x_norm_t = sb("x_norm_t", [P, KD, TOK])
        u_rows = sb("u_rows", [P, CH, T])
        pairs = sb("pairs", [P, T, CH, 2])
        states = sb("states", [P, CH, T])
        x_res = sb("x_res", [P, batch, dim])
        y = sb("y", [P, batch, dim])
        x1 = sb("x1", [P, batch, dim])
        x1_norm = sb("x1_norm", [P, batch, dim])
        x1_hi = sb("x1_hi", [P, KD, TOK], F32R)
        x1_lo = sb("x1_lo", [P, KD, TOK], F32R)
        NF = 3
        sigm = sb("sigm", [P, NF, TOK])
        gated = sb("gated", [P, NF, TOK])
        fused = sb("fused", [P, NF, TOK])
        fused_hi = sb("fused_hi", [P, NF, TOK], F32R)
        fused_lo = sb("fused_lo", [P, NF, TOK], F32R)
        z = sb("z", [P, batch, dim])
        stats = {w: sb(f"stats_{w}", [P, batch, 2, nc.vector.BN_STATS_DIM]) for w in "xyrz"}
        mean_var = {w: sb(f"mean_var_{w}", [P, batch, nc.vector.BN_AGGR_DIM]) for w in "xyrz"}
        var_eps = {w: sb(f"var_eps_{w}", [P, batch]) for w in "xyrz"}
        rstd = {w: sb(f"rstd_{w}", [P, batch]) for w in "xyrz"}

        preact = ps("preact", [P, 2, CH, 2])
        wide = [ps(f"wide{i}", [P, 512]) for i in range(4)]
        NG = 3
        gate_up = [ps(f"gate_up{i}", [P, 2, TOK]) for i in range(NG)]

        s_const_in = sem("s_const_in")
        s_small_in = sem("s_small_in")
        s_w_in_in = sem("s_w_in_in")
        s_w_out_in = sem("s_w_out_in")
        s_ident_in = sem("s_ident_in")
        s_raw_in = [sem(f"s_raw_in{i}") for i in range(RAW)]
        s_raw_free = [sem(f"s_raw_free{i}") for i in range(RAW)]
        s_piece_ready = sem("s_piece_ready")
        s_pool_pieces = sem("s_pool_pieces")
        s_pool_self = sem("s_pool_self")
        s_self = {w: sem(f"s_self_{w}") for w in ("x", "y", "r", "z", "fused", "pieces", "setup")}
        s_warm = sem("s_warm")
        s_setup = sem("s_setup")
        s_scale_ready = sem("s_scale_ready")
        s_quantised = sem("s_quantised")
        s_guarded = sem("s_guarded")
        s_x_in = sem("s_x_in")
        s_x_in_free = sem("s_x_in_free")
        s_mv = {w: sem(f"s_mv_{w}") for w in "xyrz"}
        s_rstd = {w: sem(f"s_rstd_{w}") for w in "xyrz"}
        s_x_norm = sem("s_x_norm")
        s_t1 = sem("s_t1")
        s_x_norm_t = sem("s_x_norm_t")
        s_x_norm_t_free = sem("s_x_norm_t_free")
        s_u_psum = sem("s_u_psum")
        s_u_rows = sem("s_u_rows")
        s_u_rows_free = sem("s_u_rows_free")
        s_pairs_u = sem("s_pairs_u")
        s_preact = sem("s_preact")
        s_state = sem("s_state")
        s_slice_done = sem("s_slice_done")
        s_slice_copied = sem("s_slice_copied")
        s_states = sem("s_states")
        s_states_free = sem("s_states_free")
        s_wide_free = [sem(f"s_wide_free{i}") for i in range(4)]
        s_gate_up_free = [sem(f"s_gate_up_free{i}") for i in range(NG)]
        s_y_psum = sem("s_y_psum")
        s_x_res = sem("s_x_res")
        s_x_res_free = sem("s_x_res_free")
        s_y_norm = sem("s_y_norm")
        s_x1 = sem("s_x1")
        s_x1_norm = sem("s_x1_norm")
        s_x1_norm_free = sem("s_x1_norm_free")
        s_t2 = sem("s_t2")
        s_x1_hi = sem("s_x1_hi")
        s_x1_split = sem("s_x1_split")
        s_x1_split_free = sem("s_x1_split_free")
        s_gate_up = sem("s_gate_up")
        s_sigm = sem("s_sigm")
        s_fused = sem("s_fused")
        s_fused_free = sem("s_fused_free")
        s_fused_split = sem("s_fused_split")
        s_fused_split_free = sem("s_fused_split_free")
        s_z_psum = sem("s_z_psum")
        s_z_norm = sem("s_z_norm")
        s_out_ready = sem("s_out_ready")
        s_out_stored = sem("s_out_stored")

        def ln_stats(q, slot, w, src, b):
            for half in range(2):
                def halves(eng, n, half=half):
                    eng.bn_stats(stats[w][:, b, half, :], src[:, b, half * HALF:(half + 1) * HALF]).then_inc(
                        s_self[w], 1)
                q.add("vector", slot + half, halves)

            def aggregate(eng, n):
                take(eng, s_self[w], 2)
                eng.bn_aggr(mean_var[w][:, b, :], stats[w][:, b, :, :].rearrange("p h s -> p (h s)")).then_inc(
                    s_mv[w], 1)
            q.add("vector", slot + 2, aggregate)

            def root(eng, n):
                take(eng, s_mv[w])
                eng.tensor_scalar(var_eps[w][:, b:b + 1], mean_var[w][:, b, 1:2], LN_EPS, 1.0, ALU.add,
                                  ALU.mult).then_inc(s_pool_self, 1)
                take(eng, s_pool_self)
                eng.tensor_tensor(rstd[w][:, b:b + 1], var_eps[w][:, b:b + 1], minus_half[:, 0:1],
                                  ALU.pow).then_inc(s_rstd[w], 1)
            q.add("gpsimd", slot + 2, root)

        def ln_apply(eng, w, dst, src, b):
            take(eng, s_rstd[w])
            return eng.tensor_scalar(dst[:, b, :], src[:, b, :], mean_var[w][:, b, 0:1], rstd[w][:, b:b + 1],
                                     ALU.subtract, ALU.mult)

        def setup(q):
            def loads(eng, n):
                eng.dma_start(x_in[:, :, :], x_blocks[0]).then_inc(s_x_in, 16)
                eng.dma_start(ident[:, :], identity).then_inc(s_ident_in, 16)
                eng.dma_start(cols[:, 0, :], b_in).then_inc(s_small_in, 16)
                eng.dma_start(cols[:, 1, :], beta).then_inc(s_small_in, 16)
                eng.dma_start(cols[:, 2, :], gamma).then_inc(s_small_in, 16)
                eng.dma_start(gate_scale_raw[:, :], gate_scale).then_inc(s_const_in, 16)
                eng.dma_start(up_scale_sb[:, :], up_scale).then_inc(s_const_in, 16)
                eng.dma_start(w_in_sb[:, :, :], w_in_t.rearrange("(k p) h -> p k h", p=P)).then_inc(s_w_in_in, 16)
            q.add("sync", 0, loads)

            def late_loads(eng, n):
                eng.dma_start(b_out_rows[:, :], b_out.to_broadcast([P, dim])).then_inc(s_const_in, 16)
                eng.dma_start(down_scale_rows[:, :], down_scale.to_broadcast([P, dim])).then_inc(s_const_in, 16)
                eng.dma_start(w_out_sb[:, :, :], w_out_t.rearrange("(k p) d -> p k d", p=P)).then_inc(s_w_out_in, 16)
            q.add("sync", 1, late_loads)

            def first_vector(eng, n):
                eng.memset(warm[:, :], 0.0).then_inc(s_warm, 1)
                eng.memset(factors[:, :, :], 0.0).then_inc(s_self["setup"], 1)
                eng.memset(pairs[:, 0, :, :], 0.0).then_inc(s_self["setup"], 1)
                take(eng, s_self["setup"], 2)
                pass_on(eng, s_setup)
            q.add("vector", 0, first_vector)

            def first_pool(eng, n):
                eng.memset(minus_half[:, :], -0.5).then_inc(s_pool_self, 1)
                take(eng, s_pool_self)
                take(eng, s_setup)
            q.add("gpsimd", 0, first_pool)

            def small_vector(eng, n):
                take(eng, s_small_in, 48)
                eng.tensor_tensor(u_bias[:, :], cols[:, 0, :], cols[:, 1, :], ALU.add).then_inc(s_self["setup"], 1)
                for b in range(batch):
                    eng.tensor_copy(factors[:, b:CH:batch, 1], cols[:, 2, :]).then_inc(s_self["setup"], 1)
                take(eng, s_self["setup"], 1 + batch)
                pass_on(eng, s_scale_ready)
            q.add("vector", 3, small_vector)

            def warm_up(eng, n):
                take(eng, s_warm)
                eng.activation(warm[:, 0:1], warm[:, 1:2], ACT.Sigmoid)
                take(eng, s_scale_ready)
            q.add("scalar", 0, warm_up)

        def by_pool(i):
            return i % 3 != 2

        LAST_POOL_PIECE = max(i for i in range(NP) if by_pool(i))

        def convert(q, i, slot):
            src, dst = pieces[i]
            r = i % RAW
            on_pool = by_pool(i)

            def load(eng, n):
                take(eng, s_raw_free[r])
                eng.dma_start(raw[:, r, :], src).then_inc(s_raw_in[r], 16)
            q.add("sync", slot, load)

            def binade(eng, n):
                take(eng, s_raw_in[r], 16)
                eng.tensor_scalar(rounder[:, r, :].bitcast(I32), raw[:, r, :].bitcast(I32), EXPONENT_BITS, None,
                                  ALU.bitwise_and).then_inc(s_self["pieces"], 1)
            q.add("vector", slot, binade)

            def peak(eng, n):
                eng.tensor_reduce(peaks[:, i:i + 1], raw[:, r, :], AX_X, ALU.max,
                                  apply_absolute_value=True).then_inc(s_self["pieces"], 1)
            q.add("vector", slot + 1, peak)

            def constant(eng, n):
                take(eng, s_self["pieces"], 2)
                eng.tensor_scalar(rounder[:, r, :], rounder[:, r, :], LEAST_NORMAL, ROUNDING_CONSTANT, ALU.max,
                                  ALU.mult).then_inc(s_piece_ready if on_pool else s_self["pieces"], 1)
            q.add("vector", slot + 2, constant)

            def add_constant(eng, n):
                me = s_pool_self if on_pool else s_self["pieces"]
                take(eng, s_piece_ready if on_pool else s_self["pieces"])
                eng.tensor_tensor(raw[:, r, :], raw[:, r, :], rounder[:, r, :], ALU.add).then_inc(me, 1)

            def take_off(eng, n):
                me = s_pool_self if on_pool else s_self["pieces"]
                take(eng, me)
                ins = eng.tensor_tensor(dst, raw[:, r, :], rounder[:, r, :], ALU.subtract)
                if i < NP - RAW:
                    ins.then_inc(s_raw_free[r], 1)
                else:
                    ins.then_inc(me, 1)
                    take(eng, me)
                    if i == LAST_POOL_PIECE:
                        pass_on(eng, s_pool_pieces)
            who = "gpsimd" if on_pool else "vector"
            q.add(who, slot + 3, add_constant)
            q.add(who, slot + (3 if on_pool else 4), take_off)

        def finish_weights(q, slot):
            def steps(eng, n):
                def step(ins):
                    ins.then_inc(s_self["pieces"], 1)
                    take(eng, s_self["pieces"])
                step(eng.tensor_reduce(guard[:, 0:1], peaks[:, :], AX_X, ALU.max))
                step(eng.tensor_scalar(guard[:, 1:2], guard[:, 0:1], E4M3FN_OVERFLOW, E4M3FN_OVERFLOW, ALU.max,
                                       ALU.subtract))
                step(eng.tensor_scalar(guard[:, 2:3], guard[:, 1:2], HUGE, HUGE, ALU.mult, ALU.mult))
                step(eng.tensor_scalar(guard[:, 3:4], guard[:, 2:3], 0.0, None, ALU.mult))
                step(eng.tensor_scalar(gate_scale_sb[:, :], gate_scale_raw[:, :], guard[:, 3:4], None, ALU.add))
                pass_on(eng, s_guarded)
                take(eng, s_pool_pieces)
                pass_on(eng, s_quantised)
            q.add("vector", slot, steps)

        def before(q, at, load_next, first=False):
            for b in range(batch):
                if b == 0:
                    def arrived(eng, n):
                        take(eng, s_x_in, 16)
                    q.add("vector", at["ln1"], arrived)
                ln_stats(q, at["ln1"] + 3 * b, "x", x_in, b)
            for b in range(batch):
                def norm(eng, n, b=b):
                    ln_apply(eng, "x", x_in, x_in, b).then_inc(s_x_norm, 1)
                q.add("vector", at["ln1"] + 10 + 2 * b, norm)
            if load_next is not None:
                def load(eng, n):
                    take(eng, s_x_in_free)
                    if isinstance(n, int):
                        src = x_blocks[load_next(n)]
                    else:
                        src = x_blocks[bass.ds(load_next(n), 1)].rearrange("o t b d -> (o t) b d")
                    eng.dma_start(x_in[:, :, :], src).then_inc(s_x_in, 16)
                q.add("sync", at["t1"] + 5, load)
            for b in range(batch):
                bank = 2 + b

                def transposes(eng, n, b=b, bank=bank):
                    if first and b == 0:
                        take(eng, s_ident_in, 16)
                    take(eng, s_x_norm)
                    take(eng, s_wide_free[bank])
                    for k in range(KD):
                        ins = eng.transpose(wide[bank][:, k * P:(k + 1) * P], x_in[:, b, k * P:(k + 1) * P],
                                            ident[:, :])
                    ins.then_inc(s_t1, 1)
                q.add("tensor", at["t1"] + b, transposes)
                for half in range(2):
                    def copy(eng, n, b=b, bank=bank, half=half):
                        if half == 0:
                            take(eng, s_t1)
                            if b == 0:
                                take(eng, s_x_norm_t_free)
                            if b == batch - 1:
                                pass_on(eng, s_x_in_free)
                        ks = slice(half * KD // 2, (half + 1) * KD // 2)
                        ins = eng.copy(x_norm_t[:, ks, b * P:(b + 1) * P],
                                       wide[bank][:, half * HALF:(half + 1) * HALF].rearrange(
                                           "p (k t) -> p k t", t=P))
                        if half == 1:
                            ins.then_inc(s_x_norm_t, 1)
                    q.add("scalar", at["t1"] + 3 + 2 * b + half, copy)
            for m in range(KH // 2):
                bank = m % 2

                def project(eng, n, m=m, bank=bank):
                    if m == 0:
                        if first:
                            take(eng, s_w_in_in, 16)
                        take(eng, s_x_norm_t, batch)
                        for b in range(batch):
                            pass_on(eng, s_wide_free[2 + b])
                    take(eng, s_wide_free[bank])
                    for jj in range(2):
                        j = 2 * m + jj
                        for k in range(KD):
                            ins = eng.matmul(wide[bank][:, jj * TOK:(jj + 1) * TOK],
                                             w_in_sb[:, k, j * P:(j + 1) * P], x_norm_t[:, k, :],
                                             start=(k == 0), stop=(k == KD - 1))
                    ins.then_inc(s_u_psum, 1)
                q.add("tensor", at["u"] + 7 * m, project)
                for jj in range(2):
                    def add_bias(eng, n, m=m, bank=bank, jj=jj):
                        j = 2 * m + jj
                        if jj == 0:
                            take(eng, s_u_psum)
                            if m == 0:
                                take(eng, s_u_rows_free)
                            if m == KH // 2 - 1:
                                pass_on(eng, s_x_norm_t_free)
                        ins = eng.activation(u_rows[:, j * batch:(j + 1) * batch, :].rearrange("p b t -> p (b t)"),
                                             wide[bank][:, jj * TOK:(jj + 1) * TOK], ACT.Identity,
                                             bias=u_bias[:, j:j + 1])
                        if jj == 1:
                            ins.then_inc(s_wide_free[bank] if m < KH // 2 - 1 else s_u_rows, 1)
                    q.add("scalar", at["u"] + 7 * (m + 1) + jj, add_bias)

            def relay_u(eng, n):
                take(eng, s_u_rows)
                pass_on(eng, s_wide_free[(KH // 2 - 1) % 2])
            q.add("gpsimd", at["pairs"], relay_u)

        def place_u(q, slot, s):
            def place(eng, n):
                ts = slice(s * TS, (s + 1) * TS)
                ins = eng.tensor_scalar(pairs[:, ts, :, 1].rearrange("p t c -> p c t"), u_rows[:, :, ts], 0.0, 1.0,
                                          ALU.add, ALU.mult)
                if s < SLICES - 1:
                    ins.then_inc(s_pairs_u, 1)
                else:
                    ins.then_inc(s_pool_self, 1)
                    take(eng, s_pool_self)
                    pass_on(eng, s_pairs_u)
                    pass_on(eng, s_u_rows_free)
            q.add("gpsimd", slot, place)

        def recurrence(q):
            for t in range(T):
                def pre_activation(eng, n, t=t):
                    if t:
                        eng.wait_ge(s_state, t)
                    if t % TS == 0:
                        if t:
                            pass_on(eng, s_slice_done)
                        take(eng, s_pairs_u)
                    eng.tensor_tensor_scan(preact[:, t % 2, :, :].rearrange("p c k -> p (c k)"),
                                           factors[:, :, :].rearrange("p c k -> p (c k)"),
                                           pairs[:, t, :, :].rearrange("p c k -> p (c k)"), 0.0, ALU.mult,
                                           ALU.add).then_inc(s_preact, 1)
                q.add("vector", t, pre_activation, rank=-2)

                def state(eng, n, t=t):
                    if t % TS == 0:
                        take(eng, s_slice_copied)
                    eng.wait_ge(s_preact, t + 1)
                    eng.activation(pairs[:, (t + 1) % T, :, 0], preact[:, t % 2, :, 1], ACT.Tanh).then_inc(s_state, 1)
                q.add("scalar", t, state, rank=-1)

            def end_vector(eng, n):
                take(eng, s_state, T)
                pass_on(eng, s_slice_done)
            q.add("vector", T, end_vector, rank=2)
            q.add("scalar", T, lambda eng, n: eng.sem_inc(s_preact, -T), rank=2)

        def copy_states(q, slot, s):
            def collect(eng, n):
                take(eng, s_slice_done)
                if s == 0:
                    take(eng, s_states_free)
                first, last = s * TS + 1, (s + 1) * TS + 1
                end = min(last, T)
                ins = eng.tensor_scalar(states[:, :, first - 1:end - 1],
                                        pairs[:, first:end, :, 0].rearrange("p t c -> p c t"), 0.0, 1.0, ALU.add,
                                        ALU.mult)
                if last > T:
                    ins = eng.tensor_scalar(states[:, :, T - 1:T],
                                            pairs[:, 0:1, :, 0].rearrange("p t c -> p c t"), 0.0, 1.0, ALU.add,
                                            ALU.mult)
                    ins.then_inc(s_pool_self, 1)
                    take(eng, s_pool_self)
                    pass_on(eng, s_states)
                    pass_on(eng, s_slice_copied)
                else:
                    ins.then_inc(s_slice_copied, 1)
            q.add("gpsimd", slot, collect)

        def after(q, at, first=False):
            def load_residual(eng, n):
                take(eng, s_x_res_free)
                if isinstance(n, int):
                    src = x_blocks[n - 1]
                else:
                    src = x_blocks[bass.ds(n - 1, 1)].rearrange("o t b d -> (o t) b d")
                eng.dma_start(x_res[:, :, :], src).then_inc(s_x_res, 16)
            q.add("sync", 0, load_residual)
            for b in range(batch):
                start = at["y"] + 15 * b

                def project(eng, n, b=b):
                    if b == 0:
                        if first:
                            take(eng, s_w_out_in, 16)
                        take(eng, s_states)
                    take(eng, s_wide_free[b])
                    for j in range(KH):
                        ins = eng.matmul(wide[b][:, :], states[:, j * batch + b, :], w_out_sb[:, j, :],
                                         start=(j == 0), stop=(j == KH - 1))
                    ins.then_inc(s_y_psum, 1)
                q.add("tensor", start, project)
                for half in range(2):
                    def add_bias(eng, n, b=b, half=half):
                        hs = slice(half * HALF, (half + 1) * HALF)
                        if half == 0:
                            take(eng, s_y_psum)
                            if b == batch - 1:
                                pass_on(eng, s_states_free)
                        eng.tensor_tensor(y[:, b, hs], wide[b][:, hs], b_out_rows[:, hs],
                                          ALU.add).then_inc(s_self["y"], 1)
                    q.add("vector", start + 16 + half, add_bias)

                def free_bank(eng, n, b=b):
                    take(eng, s_self["y"], 2)
                    pass_on(eng, s_wide_free[b])
                q.add("vector", start + 18, free_bank)
                ln_stats(q, start + 18, "y", y, b)

                def norm(eng, n, b=b):
                    ln_apply(eng, "y", y, y, b).then_inc(s_y_norm, 1)
                q.add("vector", start + 24, norm)

                def residual(eng, n, b=b):
                    take(eng, s_y_norm)
                    if b == 0:
                        take(eng, s_x_res, 16)
                    eng.tensor_tensor(x1[:, b, :], y[:, b, :], x_res[:, b, :], ALU.add).then_inc(s_x1, 1)
                q.add("gpsimd", start + 24, residual)

                def arrived(eng, n, b=b):
                    take(eng, s_x1)
                    if b == batch - 1:
                        pass_on(eng, s_x_res_free)
                q.add("vector", start + 28, arrived)
                ln_stats(q, start + 28, "r", x1, b)

                def norm2(eng, n, b=b):
                    take(eng, s_x1_norm_free)
                    ln_apply(eng, "r", x1_norm, x1, b).then_inc(s_x1_norm, 1)
                q.add("vector", start + 34, norm2)
                bank = 2 + b
                t2 = at["t2"][b]

                def transposes(eng, n, b=b, bank=bank):
                    take(eng, s_x1_norm)
                    take(eng, s_wide_free[bank])
                    for k in range(KD):
                        ins = eng.transpose(wide[bank][:, k * P:(k + 1) * P], x1_norm[:, b, k * P:(k + 1) * P],
                                            ident[:, :])
                    ins.then_inc(s_t2, 1)
                q.add("tensor", t2, transposes)
                for half in range(2):
                    ks = slice(half * KD // 2, (half + 1) * KD // 2)

                    def high(eng, n, b=b, bank=bank, half=half, ks=ks):
                        if half == 0:
                            take(eng, s_t2)
                            pass_on(eng, s_x1_norm_free)
                            if b == 0:
                                take(eng, s_x1_split_free)
                        eng.copy(x1_hi[:, ks, b * P:(b + 1) * P],
                                 wide[bank][:, half * HALF:(half + 1) * HALF].rearrange("p (k t) -> p k t", t=P)
                                 ).then_inc(s_x1_hi, 1)
                    q.add("scalar", t2 + 2 + half, high)
                for half in range(2):
                    ks = slice(half * KD // 2, (half + 1) * KD // 2)

                    def low(eng, n, b=b, bank=bank, half=half, ks=ks):
                        if half == 0:
                            take(eng, s_x1_hi, 2)
                        ins = eng.tensor_tensor(
                            x1_lo[:, ks, b * P:(b + 1) * P],
                            wide[bank][:, half * HALF:(half + 1) * HALF].rearrange("p (k t) -> p k t", t=P),
                            x1_hi[:, ks, b * P:(b + 1) * P].bitcast(F32), ALU.subtract)
                        if half == 1:
                            ins.then_inc(s_x1_split, 1)
                    q.add("vector", t2 + 4 + half, low)

            def gate_up_chunk(i):
                g = i % NG
                slot = at["ffn"] + int(i * at["chunk"])

                def products(eng, n):
                    if i == 0:
                        take(eng, s_x1_split, batch)
                        for b in range(batch):
                            pass_on(eng, s_wide_free[2 + b])
                        if first:
                            take(eng, s_quantised)
                    take(eng, s_gate_up_free[g])
                    for v, w_q in enumerate((gate_q, up_q)):
                        for k in range(KD):
                            for part in (x1_hi, x1_lo):
                                ins = eng.matmul(gate_up[g][:, v, :], w_q[:, k, i * P:(i + 1) * P], part[:, k, :],
                                                 start=(k == 0 and part is x1_hi),
                                                 stop=(k == KD - 1 and part is x1_lo))
                    ins.then_inc(s_gate_up, 1)
                q.add("tensor", slot, products)

                f = i % NF

                def sigmoid(eng, n):
                    if first and i == 0:
                        take(eng, s_guarded)
                    take(eng, s_gate_up)
                    if i == KI - 1:
                        pass_on(eng, s_x1_split_free)
                    eng.activation(sigm[:, f, :], gate_up[g][:, 0, :], ACT.Sigmoid,
                                   scale=gate_scale_sb[:, i:i + 1]).then_inc(s_sigm, 1)
                q.add("scalar", slot + 5, sigmoid)

                def silu(eng, n):
                    take(eng, s_sigm)
                    eng.scalar_tensor_tensor(out=gated[:, f, :], in0=gate_up[g][:, 0, :],
                                             scalar=gate_scale_sb[:, i:i + 1], in1=sigm[:, f, :], op0=ALU.mult,
                                             op1=ALU.mult).then_inc(s_self["fused"], 1)
                q.add("vector", slot + 6, silu)

                def times_up(eng, n):
                    take(eng, s_self["fused"])
                    take(eng, s_fused_free)
                    eng.scalar_tensor_tensor(out=fused[:, f, :], in0=gate_up[g][:, 1, :],
                                             scalar=up_scale_sb[:, i:i + 1], in1=gated[:, f, :], op0=ALU.mult,
                                             op1=ALU.mult).then_inc(s_fused, 1)
                q.add("vector", slot + 7, times_up)

                def split(eng, n):
                    take(eng, s_fused)
                    pass_on(eng, s_gate_up_free[g])
                    take(eng, s_fused_split_free)
                    eng.tensor_scalar(fused_hi[:, f, :], fused[:, f, :], 0.0, 1.0, ALU.add,
                                      ALU.mult).then_inc(s_pool_self, 1)
                    take(eng, s_pool_self)
                    eng.tensor_tensor(fused_lo[:, f, :], fused[:, f, :], fused_hi[:, f, :].bitcast(F32),
                                      ALU.subtract).then_inc(s_pool_self, 1)
                    take(eng, s_pool_self)
                    pass_on(eng, s_fused_free)
                    pass_on(eng, s_fused_split)
                q.add("gpsimd", slot + 7, split)

            def down_chunk(i, slot):
                f = i % NF

                def products(eng, n):
                    take(eng, s_fused_split)
                    for b in range(batch):
                        if i == 0:
                            take(eng, s_wide_free[2 + b])
                        for part in (fused_hi, fused_lo):
                            ins = eng.matmul(wide[2 + b][:, :], part[:, f, b * P:(b + 1) * P], down_q[:, i, :],
                                             start=(i == 0 and part is fused_hi),
                                             stop=(i == KI - 1 and part is fused_lo))
                        if i == KI - 1:
                            ins.then_inc(s_z_psum, 1)
                    if i < KI - 1:
                        ins.then_inc(s_fused_split_free, 1)
                q.add("tensor", slot, products)

            LAG = 2
            for i in range(KI):
                gate_up_chunk(i)
                if i >= LAG:
                    down_chunk(i - LAG, at["ffn"] + int(i * at["chunk"]) + 2)
            for i in range(KI - LAG, KI):
                down_chunk(i, at["ffn"] + int((KI - 1) * at["chunk"]) + 8)

        def tail(q, start):
            for b in range(batch):
                at_b = start + 6 * b
                for half in range(2):
                    def rescale(eng, n, b=b, half=half):
                        hs = slice(half * HALF, (half + 1) * HALF)
                        if half == 0 and b == 0:
                            take(eng, s_out_stored, 16)
                        if half == 0:
                            take(eng, s_z_psum)
                            if b == batch - 1:
                                pass_on(eng, s_fused_split_free)
                        eng.tensor_tensor(z[:, b, hs], wide[2 + b][:, hs], down_scale_rows[:, hs],
                                          ALU.mult).then_inc(s_self["z"], 1)
                    q.add("vector", at_b + half, rescale)

                def free_bank(eng, n, b=b):
                    take(eng, s_self["z"], 2)
                    pass_on(eng, s_wide_free[2 + b])
                q.add("vector", at_b + 2, free_bank)
                ln_stats(q, at_b + 2, "z", z, b)

                def norm(eng, n, b=b):
                    ln_apply(eng, "z", z, z, b).then_inc(s_z_norm, 1)
                q.add("vector", at_b + 9, norm)

                def residual(eng, n, b=b):
                    take(eng, s_z_norm)
                    ins = eng.tensor_tensor(z[:, b, :], z[:, b, :], x1[:, b, :], ALU.add)
                    if b == batch - 1:
                        ins.then_inc(s_out_ready, 1)
                q.add("gpsimd", at_b + 9, residual)

            def store(eng, n):
                take(eng, s_out_ready)
                if isinstance(n, int):
                    dst = out_blocks[n - 2]
                else:
                    dst = out_blocks[bass.ds(n - 2, 1)].rearrange("o t b d -> (o t) b d")
                eng.dma_start(dst, z[:, :, :]).then_inc(s_out_stored, 16)
            q.add("sync", start + 16, store)

        AT_BEFORE = {"ln1": 14, "t1": 30, "u": 33, "pairs": 62}
        AT_AFTER = {"y": 0, "t2": (47, 61), "ffn": 63, "chunk": 5.2}
        START_BEFORE = {"ln1": 0, "t1": 20, "u": 22, "pairs": 60}

        def period(n, scan, next_block, last_block, finished, load_next=None, pieces_at=None):
            q = Queue()
            if last_block:
                copy_states(q, 0, SLICES - 1)
            if scan:
                place_u(q, 0, SLICES - 1)
                recurrence(q)
                for s in range(SLICES - 1):
                    copy_states(q, (s + 1) * TS, s)
            if finished:
                tail(q, 1)
            if next_block:
                before(q, AT_BEFORE, load_next)
                for s in range(SLICES - 1):
                    place_u(q, max(AT_BEFORE["pairs"], (s + 1) * TS), s)
            if last_block:
                after(q, AT_AFTER, first=(n == 1))
            if pieces_at:
                for i, slot in pieces_at:
                    convert(q, i, slot)
            return q

        start = Queue()
        setup(start)
        before(start, START_BEFORE, lambda n: 1, first=True)
        for s in range(SLICES - 1):
            place_u(start, START_BEFORE["pairs"], s)
        EARLY = 10
        for i in range(EARLY):
            convert(start, i, 22 + 5 * i)

        def first_period():
            q = period(0, True, True, False, False, lambda n: 2)
            for i in range(EARLY, NP):
                convert(q, i, int((i - EARLY) * 4.6))
            return q

        periods = [(start, 0, 1), (first_period(), 0, 1)]
        second = period(1, True, True, True, False, lambda n: n + 2)
        second.add("vector", 0, lambda eng, n: take(eng, s_const_in, 64), rank=-3)
        finish_weights(second, 20)
        periods.append((second, 1, 1))
        periods.append((period(2, True, True, True, True, lambda n: n + 2), 2, NB - 4))
        periods.append((period(NB - 2, True, True, True, True), NB - 2, 1))
        periods.append((period(NB - 1, True, False, True, True), NB - 1, 1))
        periods.append((period(NB, False, False, True, True), NB, 1))
        periods.append((period(NB + 1, False, False, False, True), NB + 1, 1))

        def run(name, eng):
            for q, n, turns in periods:
                if turns == 1:
                    q.emit(name, eng, n)
                else:
                    with eng.Fori(n, n + turns) as turn:
                        q.emit(name, eng, turn)

        block = ctx.enter_context(nc.Block())

        @block.sync
        def _(eng):
            for s in s_raw_free + [s_x_res_free]:
                eng.sem_inc(s, 1)
            run("sync", eng)
            take(eng, s_out_stored, 16)

        @block.tensor
        def _(eng):
            for s in s_wide_free + s_gate_up_free:
                eng.sem_inc(s, 1)
            run("tensor", eng)

        @block.vector
        def _(eng):
            for s, count in ((s_x1_norm_free, batch), (s_fused_free, NF), (s_out_stored, 16)):
                eng.sem_inc(s, count)
            run("vector", eng)

        @block.scalar
        def _(eng):
            for s, count in ((s_x_norm_t_free, 1), (s_u_rows_free, 1), (s_x1_split_free, 1),
                             (s_slice_copied, SLICES)):
                eng.sem_inc(s, count)
            run("scalar", eng)

        @block.gpsimd
        def _(eng):
            for s, count in ((s_states_free, 1), (s_fused_split_free, NF)):
                eng.sem_inc(s, count)
            run("gpsimd", eng)


def kernel(**inputs):
    import numpy as _np
    import concourse.bacc as _bacc
    from concourse import mybir as _mybir
    from concourse.bass_utils import run_bass_kernel_spmd as _run

    a = {name: _np.asarray(value) for name, value in inputs.items()}

    def columns(v):
        return _np.ascontiguousarray(v.reshape(-1, P).T)

    arrays = {
        "x": a["L0_attn_x"],
        "w_in_t": a["L0_attn_W_in"].T,
        "w_out_t": a["L0_attn_W_out"].T,
        "b_in": columns(a["L0_attn_b_in"]),
        "beta": columns(a["L0_attn_beta"]),
        "gamma": columns(a["L0_attn_gamma"]),
        "b_out": a["L0_attn_b_out"].reshape(1, -1),
        "gate_w": a["L0_ffn_gate_w"],
        "up_w": a["L0_ffn_up_w"],
        "down_w": a["L0_ffn_down_w"],
        "gate_scale": columns(a["L0_ffn_gate_scale"]),
        "up_scale": columns(a["L0_ffn_up_scale"]),
        "down_scale": a["L0_ffn_down_scale"].reshape(1, -1),
        "identity": _np.eye(P, dtype=_np.float32),
    }
    arrays = {name: _np.ascontiguousarray(value) for name, value in arrays.items()}
    nc = _bacc.Bacc("TRN2", target_bir_lowering=False, num_devices=1)
    args = [nc.dram_tensor(name, v.shape, _mybir.dt.from_np(v.dtype), kind="ExternalInput").ap()
            for name, v in arrays.items()]
    shape = a["L0_attn_x"].shape
    args.append(nc.dram_tensor("out", shape, _mybir.dt.float32, kind="ExternalOutput").ap())
    recurrent_sandwich_kernel(nc, *args)
    r = _run(nc, [arrays], core_ids=[0])
    return r.results[0]["out"]
```

```python
from contextlib import ExitStack

import concourse.bass as bass
from concourse import mybir

P = 128
F32 = mybir.dt.float32
F32R = mybir.dt.float32r
I32 = mybir.dt.int32
ALU = mybir.AluOpType
ACT = mybir.ActivationFunctionType
AX_X = mybir.AxisListType.X
LN_EPS = 1e-5

EXPONENT_BITS = 0x7F800000
LEAST_NORMAL = 2.0 ** -6
ROUNDING_CONSTANT = 1.5 * 2.0 ** 20
E4M3FN_OVERFLOW = 464.0
HUGE = 1e38


class Queue:

    def __init__(self):
        self.items = {"sync": [], "tensor": [], "vector": [], "scalar": [], "gpsimd": []}
        self.added = 0

    def add(self, engine, slot, emit, rank=1):
        self.added += 1
        self.items[engine].append((slot, rank, self.added, emit))

    def free_slots(self, engine, first, end):
        used = {int(slot) for slot, rank, _, _ in self.items[engine] if rank == 1}
        return iter([slot for slot in range(first, end) if slot not in used])

    def emit(self, engine, eng, n):
        for _, _, _, emit in sorted(self.items[engine], key=lambda item: item[:3]):
            emit(eng, n)
        take_out(eng)


TAKEN = {}


def take(eng, sem, count=1):
    seen = TAKEN.get(sem.name, (0, sem))[0] + count
    TAKEN[sem.name] = (seen, sem)
    eng.wait_ge(sem, seen)


def take_out_one(eng):
    if TAKEN:
        seen, sem = TAKEN.pop(next(iter(TAKEN)))
        eng.sem_inc(sem, -seen)


def take_out(eng):
    while TAKEN:
        take_out_one(eng)


def pass_on(eng, sem):
    eng.sem_inc(sem, 1)


def recurrent_sandwich_kernel(nc, x, w_in_t, w_out_t, b_in, beta, gamma, b_out, gate_w, up_w, down_w,
                              gate_scale, up_scale, down_scale, identity, out):
    batch, seq, dim = x.shape
    hidden = w_in_t.shape[1]
    inner = gate_w.shape[1]
    KD = dim // P
    KH = hidden // P
    KI = inner // P
    T = 128
    NB = seq // T
    CH = KH * batch
    TOK = batch * T
    SLICES = 4
    TS = T // SLICES
    HALF = dim // 2
    GROUPS = batch
    TH = T // GROUPS
    QUADS = KH // 4
    assert T == P and TOK == 256 and dim == 512 and seq % T == 0

    x_blocks = x.rearrange("b (n t) d -> n t b d", t=T)
    out_blocks = out.rearrange("b (n t) d -> n t b d", t=T)

    with ExitStack() as ctx:
        def sb(name, shape, dt=F32):
            return ctx.enter_context(nc.sbuf_tensor(name, shape, dt))

        def ps(name, shape):
            return ctx.enter_context(nc.psum_tensor(name, shape, F32))

        def sem(name):
            return ctx.enter_context(nc.semaphore(name))

        w_in_sb = sb("w_in_sb", [P, KD, hidden])
        w_out_sb = sb("w_out_sb", [P, KH, dim])
        gate_q = sb("gate_q", [P, KD, inner], F32R)
        up_q = sb("up_q", [P, KD, inner], F32R)
        down_q = sb("down_q", [P, KI, dim], F32R)
        ident = sb("ident", [P, P])
        b_out_rows = sb("b_out_rows", [P, dim])
        down_scale_rows = sb("down_scale_rows", [P, dim])
        cols = sb("cols", [P, 3, KH])
        u_bias = sb("u_bias", [P, KH])
        gate_scale_cols = sb("gate_scale_cols", [P, KI])
        up_scale_sb = sb("up_scale_sb", [P, KI])
        minus_half = sb("minus_half", [P, 2])
        warm = sb("warm", [P, 2])
        factors = sb("factors", [P, CH, 2])

        OWN = 3
        raw_own = sb("raw_own", [P, OWN, dim])
        rounder_own = sb("rounder_own", [P, OWN, dim])
        pieces = []
        for k in range(KD):
            for w_dram, w_q in ((gate_w, gate_q), (up_w, up_q)):
                for c in range(inner // dim):
                    pieces.append((w_dram[k * P:(k + 1) * P, c * dim:(c + 1) * dim],
                                   w_q[:, k, c * dim:(c + 1) * dim]))
        for i in range(KI):
            pieces.append((down_w[i * P:(i + 1) * P, :], down_q[:, i, :]))
        NP = len(pieces)
        peaks = sb("peaks", [P, NP, 2])
        guard = sb("guard", [P, 3])

        x_in = sb("x_in", [P, batch, dim])
        x_norm_t = sb("x_norm_t", [P, KD, TOK])
        u_rows = sb("u_rows", [P, CH, T])
        pairs = sb("pairs", [P, T, CH, 2])
        states = sb("states", [P, CH, T])
        x_res = sb("x_res", [P, batch, dim])
        y = sb("y", [P, batch, dim])
        x1 = sb("x1", [P, batch, dim])
        x1_norm = sb("x1_norm", [P, batch, dim])
        x1_hi = sb("x1_hi", [P, KD, TOK], F32R)
        x1_lo = sb("x1_lo", [P, KD, TOK], F32R)
        NF = 3
        sigm = sb("sigm", [P, NF, TOK])
        gated = sb("gated", [P, NF, TOK])
        fused = sb("fused", [P, NF, TOK])
        fused_hi = sb("fused_hi", [P, NF, TOK], F32R)
        fused_lo = sb("fused_lo", [P, NF, TOK], F32R)
        z = sb("z", [P, batch, dim])
        RAW = OWN + 1
        raw = [raw_own[:, r, :] for r in range(OWN)] + [z[:, 0, :]]
        rounder = [rounder_own[:, r, :] for r in range(OWN)] + [z[:, 1, :]]
        stats = {w: sb(f"stats_{w}", [P, batch, 2, nc.vector.BN_STATS_DIM]) for w in "xyrz"}
        mean_var = {w: sb(f"mean_var_{w}", [P, batch, nc.vector.BN_AGGR_DIM]) for w in "xyrz"}
        var_eps = {w: sb(f"var_eps_{w}", [P, batch]) for w in "xyrz"}
        rstd = {w: sb(f"rstd_{w}", [P, batch]) for w in "xyrz"}

        preact = ps("preact", [P, 2, CH, 2])
        wide = [ps(f"wide{i}", [P, 512]) for i in range(4)]
        NG = 3
        gate_up = [ps(f"gate_up{i}", [P, 2, TOK]) for i in range(NG)]

        s_const_in = sem("s_const_in")
        s_small_in = sem("s_small_in")
        s_w_in_in = [sem(f"s_w_in_in{m}") for m in range(KH // 2)]
        s_w_out_in = sem("s_w_out_in")
        s_ident_in = sem("s_ident_in")
        s_raw_in = [sem(f"s_raw_in{i}") for i in range(RAW)]
        s_raw_free = [sem(f"s_raw_free{i}") for i in range(RAW)]
        s_piece_ready = sem("s_piece_ready")
        s_converted = {who: sem(f"s_converted_by_{who}") for who in ("gpsimd", "vector")}
        s_pool_self = sem("s_pool_self")
        s_self = {w: sem(f"s_self_{w}") for w in ("x", "y", "r", "z", "fused", "pieces", "rounding", "setup")}
        s_scalar_self = sem("s_scalar_self")
        s_warm = sem("s_warm")
        s_setup = sem("s_setup")
        s_scale_ready = sem("s_scale_ready")
        s_guarded = sem("s_guarded")
        s_x_in = sem("s_x_in")
        s_x_in_free = sem("s_x_in_free")
        s_mv = {w: sem(f"s_mv_{w}") for w in "xyrz"}
        s_rstd = {w: sem(f"s_rstd_{w}") for w in "xyrz"}
        s_x_norm = sem("s_x_norm")
        s_t1 = sem("s_t1")
        s_x_norm_t = sem("s_x_norm_t")
        s_x_norm_t_free = sem("s_x_norm_t_free")
        s_u_psum = sem("s_u_psum")
        s_u_rows = sem("s_u_rows")
        s_u_rows_free = sem("s_u_rows_free")
        s_pairs_u = sem("s_pairs_u")
        s_preact = sem("s_preact")
        s_state = sem("s_state")
        s_slice_done = sem("s_slice_done")
        s_slice_copied = sem("s_slice_copied")
        s_states = sem("s_states")
        s_states_free = sem("s_states_free")
        s_wide_free = [sem(f"s_wide_free{i}") for i in range(4)]
        s_gate_up_free = [sem(f"s_gate_up_free{i}") for i in range(NG)]
        s_y_psum = sem("s_y_psum")
        s_x_res = sem("s_x_res")
        s_x_res_free = sem("s_x_res_free")
        s_y_norm = sem("s_y_norm")
        s_x1 = sem("s_x1")
        s_x1_norm = sem("s_x1_norm")
        s_x1_norm_free = sem("s_x1_norm_free")
        s_t2 = sem("s_t2")
        s_x1_hi = sem("s_x1_hi")
        s_x1_split = sem("s_x1_split")
        s_x1_split_free = sem("s_x1_split_free")
        s_gate_up = sem("s_gate_up")
        s_sigm = sem("s_sigm")
        s_fused = sem("s_fused")
        s_fused_hi = sem("s_fused_hi")
        s_fused_free = sem("s_fused_free")
        s_fused_split = sem("s_fused_split")
        s_fused_split_free = sem("s_fused_split_free")
        s_z_psum = sem("s_z_psum")
        s_z_norm = sem("s_z_norm")
        s_out_ready = sem("s_out_ready")
        s_out_stored = sem("s_out_stored")
        s_last_stored = sem("s_last_stored")

        def ln_stats(q, halves_at, whole_at, w, src, b):
            for half in range(2):
                def halves(eng, n, half=half):
                    eng.bn_stats(stats[w][:, b, half, :], src[:, b, half * HALF:(half + 1) * HALF]).then_inc(
                        s_self[w], 1)
                q.add("vector", halves_at[half], halves)

            def aggregate(eng, n):
                take(eng, s_self[w], 2)
                eng.bn_aggr(mean_var[w][:, b, :], stats[w][:, b, :, :].rearrange("p h s -> p (h s)")).then_inc(
                    s_mv[w], 1)
            q.add("vector", whole_at, aggregate)

            def root(eng, n):
                take(eng, s_mv[w])
                eng.tensor_scalar(var_eps[w][:, b:b + 1], mean_var[w][:, b, 1:2], LN_EPS, 1.0, ALU.add,
                                  ALU.mult).then_inc(s_pool_self, 1)
                take(eng, s_pool_self)
                eng.tensor_tensor(rstd[w][:, b:b + 1], var_eps[w][:, b:b + 1], minus_half[:, 0:1],
                                  ALU.pow).then_inc(s_rstd[w], 1)
            q.add("gpsimd", whole_at, root)

        def ln_apply(q, slot, w, dst, src, b, done, room=None):
            for half in range(2):
                def norm(eng, n, half=half, hs=slice(half * HALF, (half + 1) * HALF)):
                    if half == 0:
                        take(eng, s_rstd[w])
                        if room is not None:
                            take(eng, room)
                    eng.tensor_scalar(dst[:, b, hs], src[:, b, hs], mean_var[w][:, b, 0:1], rstd[w][:, b:b + 1],
                                      ALU.subtract, ALU.mult).then_inc(done, 1)
                q.add("vector", slot + half, norm)

        def setup(q):
            def loads(eng, n):
                for b in range(batch):
                    eng.dma_start(x_in[b * TH:(b + 1) * TH, :, :],
                                  x_blocks[0][:, b, :].rearrange("(g t) d -> t g d", g=GROUPS)).then_inc(s_x_in, 16)
                eng.dma_start(ident[:, :], identity).then_inc(s_ident_in, 16)
                eng.dma_start(cols[:, 0, :], b_in).then_inc(s_small_in, 16)
                eng.dma_start(cols[:, 1, :], beta).then_inc(s_small_in, 16)
                eng.dma_start(cols[:, 2, :], gamma).then_inc(s_small_in, 16)
                eng.dma_start(gate_scale_cols[:, :], gate_scale).then_inc(s_const_in, 16)
                eng.dma_start(up_scale_sb[:, :], up_scale).then_inc(s_const_in, 16)
                for m in range(KH // 2):
                    ms = slice(2 * m * P, 2 * (m + 1) * P)
                    eng.dma_start(w_in_sb[:, :, ms], w_in_t[:, ms].rearrange("(k p) h -> p k h", p=P)
                                  ).then_inc(s_w_in_in[m], 16)
            q.add("sync", 0, loads)

            def first_vector(eng, n):
                eng.memset(warm[:, :], 0.0).then_inc(s_warm, 1)
                eng.memset(factors[:, :, :], 0.0).then_inc(s_self["setup"], 1)
                eng.memset(pairs[:, 0, :, :], 0.0).then_inc(s_self["setup"], 1)
                take(eng, s_self["setup"], 2)
                pass_on(eng, s_setup)
            q.add("vector", 0, first_vector)

            def first_pool(eng, n):
                eng.memset(minus_half[:, :], -0.5).then_inc(s_pool_self, 1)
                take(eng, s_pool_self)
                take(eng, s_setup)
            q.add("gpsimd", 0, first_pool)

            def small_vector(eng, n):
                take(eng, s_small_in, 48)
                eng.tensor_tensor(u_bias[:, :], cols[:, 0, :], cols[:, 1, :], ALU.add).then_inc(s_self["setup"], 1)
                for b in range(batch):
                    eng.tensor_copy(factors[:, b:CH:batch, 1], cols[:, 2, :]).then_inc(s_self["setup"], 1)
                take(eng, s_self["setup"], 1 + batch)
                pass_on(eng, s_scale_ready)
            q.add("vector", 3, small_vector)

            def warm_up(eng, n):
                take(eng, s_warm)
                eng.activation(warm[:, 0:1], warm[:, 1:2], ACT.Sigmoid)
                take(eng, s_scale_ready)
            q.add("scalar", 0, warm_up)

        def late_loads(q, slots):
            def rows(eng, n):
                eng.dma_start(b_out_rows[:, :], b_out.to_broadcast([P, dim])).then_inc(s_const_in, 16)
                eng.dma_start(down_scale_rows[:, :], down_scale.to_broadcast([P, dim])).then_inc(s_const_in, 16)
            q.add("sync", slots[0], rows)
            for j in range(KH):
                def load(eng, n, j=j):
                    eng.dma_start(w_out_sb[:, j, :], w_out_t[j * P:(j + 1) * P, :]).then_inc(s_w_out_in, 16)
                q.add("sync", slots[j], load)

        GATE_UP_PIECES = NP - KI

        def by_pool(i):
            return i % 4 != 3 if i < GATE_UP_PIECES else i % 3 != 2

        LAST_POOL_GATE_UP = max(i for i in range(GATE_UP_PIECES) if by_pool(i))
        assert not by_pool(GATE_UP_PIECES - 1) and not by_pool(NP - 1)

        LOAD_AHEAD = 10
        room_at = {}

        def convert(q, i, slots):
            src, dst = pieces[i]
            r = i % RAW
            on_pool = by_pool(i)
            slot = next(slots)

            def load(eng, n):
                take(eng, s_raw_free[r])
                eng.dma_start(raw[r], src).then_inc(s_raw_in[r], 16)
            room_q, room_slot = room_at.get(i - RAW, (q, 0))
            q.add("sync", max(slot - LOAD_AHEAD, room_slot if room_q is q else -LOAD_AHEAD), load)

            def binade(eng, n):
                take(eng, s_raw_in[r], 16)
                eng.tensor_scalar(rounder[r].bitcast(I32), raw[r].bitcast(I32), EXPONENT_BITS, None,
                                  ALU.bitwise_and).then_inc(s_self["pieces"], 1)
            q.add("vector", slot, binade)

            for half in range(2):
                def peak(eng, n, hs=slice(half * HALF, (half + 1) * HALF), half=half):
                    eng.tensor_reduce(peaks[:, i, half:half + 1], raw[r][:, hs], AX_X, ALU.max,
                                      apply_absolute_value=True).then_inc(s_self["pieces"], 1)
                q.add("vector", next(slots), peak)

            def constant(eng, n):
                take(eng, s_self["pieces"], 3)
                eng.tensor_scalar(rounder[r], rounder[r], LEAST_NORMAL, ROUNDING_CONSTANT, ALU.max,
                                  ALU.mult).then_inc(s_piece_ready if on_pool else s_self["rounding"], 1)
            slot = next(slots)
            q.add("vector", slot, constant)

            who, me = ("gpsimd", s_pool_self) if on_pool else ("vector", s_self["rounding"])
            parts = 1 if on_pool else 2
            size = dim // parts
            for part in range(parts):
                def add_constant(eng, n, part=part, cs=slice(part * size, (part + 1) * size)):
                    if part == 0:
                        take(eng, s_piece_ready if on_pool else me)
                    eng.tensor_tensor(raw[r][:, cs], raw[r][:, cs], rounder[r][:, cs], ALU.add).then_inc(me, 1)
                q.add(who, slot if on_pool else next(slots), add_constant)
            for part in range(parts):
                def take_off(eng, n, part=part, cs=slice(part * size, (part + 1) * size)):
                    if part == 0:
                        take(eng, me, parts)
                    eng.tensor_tensor(dst[:, cs], raw[r][:, cs], rounder[r][:, cs], ALU.subtract).then_inc(me, 1)
                slot = slot if on_pool else next(slots)
                q.add(who, slot, take_off)

            def report(eng, n):
                take(eng, me, parts)
                if i < NP - RAW:
                    pass_on(eng, s_raw_free[r])
                if i == LAST_POOL_GATE_UP or i >= GATE_UP_PIECES:
                    pass_on(eng, s_converted[who])
            slot = slot if on_pool else next(slots)
            room_at[i] = (q, slot)
            q.add(who, slot, report)

        def guard_weights(q, slots, first, end, poisoned):
            steps = (
                lambda eng: eng.tensor_reduce(guard[:, 0:1], peaks[:, first:end, :].rearrange("p i h -> p (i h)"),
                                              AX_X, ALU.max),
                lambda eng: eng.tensor_scalar(guard[:, 1:2], guard[:, 0:1], E4M3FN_OVERFLOW, E4M3FN_OVERFLOW,
                                              ALU.max, ALU.subtract),
                lambda eng: eng.tensor_scalar(guard[:, 2:3], guard[:, 1:2], HUGE, HUGE, ALU.mult, ALU.mult),
                lambda eng: eng.scalar_tensor_tensor(out=poisoned, in0=guard[:, 2:3], scalar=0.0,
                                                     in1=poisoned.bitcast(F32), op0=ALU.mult, op1=ALU.add),
            )
            for i, step in enumerate(steps):
                def run_step(eng, n, i=i, step=step):
                    if i:
                        take(eng, s_self["setup"])
                    step(eng).then_inc(s_self["setup"], 1)
                q.add("vector", next(slots), run_step)

            def report(eng, n):
                take(eng, s_self["setup"])
                pass_on(eng, s_guarded)
            q.add("vector", next(slots), report)

        def before(q, at, load_next, first=False):
            for b in range(batch):
                if b == 0:
                    def arrived(eng, n):
                        take(eng, s_x_in, 16 * batch if first else 16)
                    q.add("vector", at["x_halves"][0][0], arrived)
                ln_stats(q, at["x_halves"][b], at["x_whole"][b], "x", x_in, b)
            for b in range(batch):
                ln_apply(q, at["x_norm"][b], "x", x_in, x_in, b, s_x_norm)
            if load_next is not None:
                def load(eng, n):
                    take(eng, s_x_in_free)
                    if isinstance(n, int):
                        src = x_blocks[load_next(n)]
                    else:
                        src = x_blocks[bass.ds(load_next(n), 1)].rearrange("o t b d -> (o t) b d")
                    eng.dma_start(x_in[:, :, :], src).then_inc(s_x_in, 16)
                q.add("sync", at["t1_copy"][-1], load)
            for b in range(batch):
                bank = gate_up[b][:, :, :].rearrange("p v t -> p (v t)")

                def transposes(eng, n, b=b, bank=bank):
                    if first and b == 0:
                        take(eng, s_ident_in, 16)
                    take(eng, s_x_norm, 2)
                    take(eng, s_gate_up_free[b])
                    for k in range(KD):
                        ins = eng.transpose(bank[:, k * P:(k + 1) * P], x_in[:, b, k * P:(k + 1) * P],
                                            ident[:, :])
                    ins.then_inc(s_t1, 1)
                q.add("tensor", at["t1"][b], transposes)
                for half in range(2):
                    def copy(eng, n, b=b, bank=bank, half=half):
                        if half == 0:
                            take(eng, s_t1)
                            if b == 0 and not first:
                                take(eng, s_x_norm_t_free)
                            if b == batch - 1:
                                pass_on(eng, s_x_in_free)
                        ks = slice(half * KD // 2, (half + 1) * KD // 2)
                        ins = eng.copy(x_norm_t[:, ks, b * P:(b + 1) * P],
                                       bank[:, half * HALF:(half + 1) * HALF].rearrange("p (k t) -> p k t", t=P))
                        if half == 1:
                            ins.then_inc(s_x_norm_t, 1)
                    q.add("scalar", at["t1_copy"][2 * b + half], copy)
            if first:
                return
            for m in range(KH // 2):
                bank = m % 2

                def project(eng, n, m=m, bank=bank):
                    if m == 0:
                        take(eng, s_x_norm_t, batch)
                        for b in range(batch):
                            pass_on(eng, s_gate_up_free[b])
                    take(eng, s_wide_free[bank])
                    for jj in range(2):
                        j = 2 * m + jj
                        for k in range(KD):
                            ins = eng.matmul(wide[bank][:, jj * TOK:(jj + 1) * TOK],
                                             w_in_sb[:, k, j * P:(j + 1) * P], x_norm_t[:, k, :],
                                             start=(k == 0), stop=(k == KD - 1))
                    ins.then_inc(s_u_psum, 1)
                q.add("tensor", at["u"][m], project)
                for jj in range(2):
                    def add_bias(eng, n, m=m, bank=bank, jj=jj):
                        j = 2 * m + jj
                        if jj == 0:
                            take(eng, s_u_psum)
                            if m == 0:
                                take(eng, s_u_rows_free)
                            if m == KH // 2 - 1:
                                pass_on(eng, s_x_norm_t_free)
                        chains = slice(j * batch, (j + 1) * batch)
                        ins = eng.activation(u_rows[:, chains, :].rearrange("p b t -> p (b t)"),
                                             wide[bank][:, jj * TOK:(jj + 1) * TOK], ACT.Identity,
                                             bias=u_bias[:, j:j + 1])
                        if jj == 1:
                            ins.then_inc(s_wide_free[bank] if m < KH // 2 - 1 else s_u_rows, 1)
                    q.add("scalar", at["u_copy"][m] + jj, add_bias)

            def relay_u(eng, n):
                take(eng, s_u_rows)
                pass_on(eng, s_wide_free[(KH // 2 - 1) % 2])
            q.add("gpsimd", at["pairs"], relay_u)

        def first_u(q, at, g):
            for quad in range(QUADS):
                bank = quad % 2

                def project(eng, n, quad=quad, bank=bank):
                    if quad == 0:
                        take(eng, s_x_norm_t)
                        pass_on(eng, s_gate_up_free[g])
                    take(eng, s_wide_free[bank])
                    for jj in range(4):
                        j = 4 * quad + jj
                        if g == 0 and jj % 2 == 0:
                            take(eng, s_w_in_in[j // 2], 16)
                        for k in range(KD):
                            ins = eng.matmul(wide[bank][:, jj * P:(jj + 1) * P], w_in_sb[:, k, j * P:(j + 1) * P],
                                             x_norm_t[:, k, g * P:(g + 1) * P], start=(k == 0), stop=(k == KD - 1))
                    ins.then_inc(s_u_psum, 1)
                q.add("tensor", at["u"][quad], project)
                for jj in range(4):
                    def add_bias(eng, n, quad=quad, bank=bank, jj=jj):
                        j = 4 * quad + jj
                        if jj == 0:
                            take(eng, s_u_psum)
                        ins = eng.activation(
                            pairs[:, g * TH:(g + 1) * TH, j * batch:(j + 1) * batch, 1].rearrange("p t b -> p b t"),
                            wide[bank][:, jj * P:(jj + 1) * P].rearrange("p (b t) -> p b t", b=batch),
                            ACT.Identity, bias=u_bias[:, j:j + 1])
                        if jj == 3:
                            ins.then_inc(s_scalar_self, 1)
                            take(eng, s_scalar_self)
                            pass_on(eng, s_wide_free[bank])
                            if quad == QUADS - 1:
                                eng.sem_inc(s_pairs_u, SLICES // GROUPS)
                    q.add("scalar", at["u_copy"][quad] + jj, add_bias)

        def place_u(q, slot, s):
            def place(eng, n):
                ts = slice(s * TS, (s + 1) * TS)
                ins = eng.tensor_scalar(pairs[:, ts, :, 1].rearrange("p t c -> p c t"), u_rows[:, :, ts], 0.0, 1.0,
                                          ALU.add, ALU.mult)
                if s < SLICES - 1:
                    ins.then_inc(s_pairs_u, 1)
                else:
                    ins.then_inc(s_pool_self, 1)
                    take(eng, s_pool_self)
                    pass_on(eng, s_pairs_u)
                    pass_on(eng, s_u_rows_free)
            q.add("gpsimd", slot, place)

        def recurrence(q):
            for t in range(T):
                def pre_activation(eng, n, t=t):
                    if t:
                        take(eng, s_state)
                    else:
                        take(eng, s_pairs_u)
                    eng.tensor_tensor_scan(preact[:, t % 2, :, :].rearrange("p c k -> p (c k)"),
                                           factors[:, :, :].rearrange("p c k -> p (c k)"),
                                           pairs[:, t, :, :].rearrange("p c k -> p (c k)"), 0.0, ALU.mult,
                                           ALU.add).then_inc(s_preact, 1)
                    if t and t % TS == 0:
                        pass_on(eng, s_slice_done)
                    if t + 1 < T and (t + 1) % TS == 0:
                        take(eng, s_pairs_u)
                    take_out_one(eng)
                q.add("vector", t, pre_activation, rank=-2)

                def state(eng, n, t=t):
                    if t == 0:
                        take(eng, s_slice_copied)
                    take(eng, s_preact)
                    eng.activation(pairs[:, (t + 1) % T, :, 0], preact[:, t % 2, :, 1], ACT.Tanh).then_inc(s_state, 1)
                    if t + 1 < T and (t + 1) % TS == 0:
                        take(eng, s_slice_copied)
                    take_out_one(eng)
                q.add("scalar", t, state, rank=-1)

            def end_vector(eng, n):
                take(eng, s_state)
                pass_on(eng, s_slice_done)
            q.add("vector", T, end_vector, rank=2)

        def copy_states(q, slot, s):
            def collect(eng, n):
                take(eng, s_slice_done)
                if s == 0:
                    take(eng, s_states_free)
                first, last = s * TS + 1, (s + 1) * TS + 1
                end = min(last, T)
                ins = eng.tensor_scalar(states[:, :, first - 1:end - 1],
                                        pairs[:, first:end, :, 0].rearrange("p t c -> p c t"), 0.0, 1.0, ALU.add,
                                        ALU.mult)
                if last > T:
                    ins = eng.tensor_scalar(states[:, :, T - 1:T],
                                            pairs[:, 0:1, :, 0].rearrange("p t c -> p c t"), 0.0, 1.0, ALU.add,
                                            ALU.mult)
                    ins.then_inc(s_pool_self, 1)
                    take(eng, s_pool_self)
                    pass_on(eng, s_states)
                    pass_on(eng, s_slice_copied)
                else:
                    ins.then_inc(s_slice_copied, 1)
            q.add("gpsimd", slot, collect)

        LAG = 3
        GATE_UP_SLOTS = 3.75
        DOWN_SLOTS = 1.87

        def down_chunk(q, i, slot, first=False):
            f = i % NF

            def products(eng, n):
                take(eng, s_fused_split)
                if first:
                    take(eng, s_converted["gpsimd" if by_pool(GATE_UP_PIECES + i) else "vector"])
                for b in range(batch):
                    if i == 0:
                        take(eng, s_wide_free[2 + b])
                    for part in (fused_hi, fused_lo):
                        ins = eng.matmul(wide[2 + b][:, :], part[:, f, b * P:(b + 1) * P], down_q[:, i, :],
                                         start=(i == 0 and part is fused_hi),
                                         stop=(i == KI - 1 and part is fused_lo))
                    if i == KI - 1:
                        ins.then_inc(s_z_psum, 1)
                if i < KI - 1:
                    ins.then_inc(s_fused_split_free, 1)
            q.add("tensor", slot, products)

        def gate_up_products(q, i, slot, first=False):
            g = i % NG

            def products(eng, n):
                if i == 0:
                    take(eng, s_x1_split, batch)
                    for b in range(batch):
                        pass_on(eng, s_wide_free[2 + b])
                    if first:
                        take(eng, s_guarded)
                        take(eng, s_converted["gpsimd"])
                take(eng, s_gate_up_free[g])
                for v, w_q in enumerate((gate_q, up_q)):
                    for k in range(KD):
                        for part in (x1_hi, x1_lo):
                            ins = eng.matmul(gate_up[g][:, v, :], w_q[:, k, i * P:(i + 1) * P], part[:, k, :],
                                             start=(k == 0 and part is x1_hi),
                                             stop=(k == KD - 1 and part is x1_lo))
                ins.then_inc(s_gate_up, 1)
            q.add("tensor", slot, products)

        def gate_up_use(q, i, sigmoid_at, silu_at, up_at, high_at):
            g = i % NG
            f = i % NF

            def sigmoid(eng, n):
                take(eng, s_gate_up)
                if i == KI - 1:
                    pass_on(eng, s_x1_split_free)
                eng.activation(sigm[:, f, :], gate_up[g][:, 0, :], ACT.Sigmoid,
                               scale=gate_scale_cols[:, i:i + 1]).then_inc(s_sigm, 1)
            q.add("scalar", sigmoid_at, sigmoid)

            def silu(eng, n):
                take(eng, s_sigm)
                eng.scalar_tensor_tensor(out=gated[:, f, :], in0=gate_up[g][:, 0, :],
                                         scalar=gate_scale_cols[:, i:i + 1], in1=sigm[:, f, :], op0=ALU.mult,
                                         op1=ALU.mult).then_inc(s_self["fused"], 1)
            q.add("vector", silu_at, silu)

            def times_up(eng, n):
                take(eng, s_self["fused"])
                take(eng, s_fused_free)
                eng.scalar_tensor_tensor(out=fused[:, f, :], in0=gate_up[g][:, 1, :],
                                         scalar=up_scale_sb[:, i:i + 1], in1=gated[:, f, :], op0=ALU.mult,
                                         op1=ALU.mult).then_inc(s_fused, 1)
            q.add("vector", up_at, times_up)

            def high(eng, n):
                take(eng, s_fused)
                pass_on(eng, s_gate_up_free[g])
                take(eng, s_fused_split_free)
                eng.copy(fused_hi[:, f, :], fused[:, f, :]).then_inc(s_fused_hi, 1)
            q.add("scalar", high_at, high)

            def low(eng, n):
                take(eng, s_fused_hi)
                eng.tensor_tensor(fused_lo[:, f, :], fused[:, f, :], fused_hi[:, f, :].bitcast(F32),
                                  ALU.subtract).then_inc(s_pool_self, 1)
                take(eng, s_pool_self)
                pass_on(eng, s_fused_free)
                pass_on(eng, s_fused_split)
            q.add("gpsimd", high_at, low)

        CHUNKS_IN_TIME = KI - 1
        DOWN_IN_TIME = CHUNKS_IN_TIME - LAG

        def ffn(q, at, whole, first=False):
            chunks = KI if whole else CHUNKS_IN_TIME
            for i in range(chunks):
                slot = at["ffn"] + GATE_UP_SLOTS * i + DOWN_SLOTS * max(0, i - LAG)
                gate_up_products(q, i, slot, first)
                if i >= LAG:
                    down_chunk(q, i - LAG, slot + GATE_UP_SLOTS, first)
                if whole or i < CHUNKS_IN_TIME - 1:
                    c = int(slot + 4.7)
                    gate_up_use(q, i, c, c + 2, c + 3, c + (5 if i < LAG else 4))
            if whole:
                for i in range(KI - LAG, KI):
                    down_chunk(q, i, slot + 6)

        def ffn_rest(q, at):
            gate_up_products(q, KI - 1, -2)
            gate_up_use(q, KI - 2, *at["next_to_last"])
            gate_up_use(q, KI - 1, *at["last"])
            for i in range(DOWN_IN_TIME, KI):
                down_chunk(q, i, -1 if i < KI - 2 else at["down"])

        def after(q, at, first=False):
            def load_residual(eng, n):
                take(eng, s_x_res_free, 2)
                if isinstance(n, int):
                    src = x_blocks[n - 1]
                else:
                    src = x_blocks[bass.ds(n - 1, 1)].rearrange("o t b d -> (o t) b d")
                eng.dma_start(x_res[:, :, :], src).then_inc(s_x_res, 16)
            q.add("sync", 0, load_residual)
            for b in range(batch):
                def project(eng, n, b=b):
                    if b == 0:
                        if first:
                            take(eng, s_w_out_in, 16 * KH)
                        take(eng, s_states)
                    take(eng, s_wide_free[b])
                    for j in range(KH):
                        ins = eng.matmul(wide[b][:, :], states[:, j * batch + b, :], w_out_sb[:, j, :],
                                         start=(j == 0), stop=(j == KH - 1))
                    ins.then_inc(s_y_psum, 1)
                q.add("tensor", at["y"][b], project)
                for half in range(2):
                    def add_bias(eng, n, b=b, half=half):
                        hs = slice(half * HALF, (half + 1) * HALF)
                        if half == 0:
                            take(eng, s_y_psum)
                            if b == batch - 1:
                                pass_on(eng, s_states_free)
                        eng.tensor_tensor(y[:, b, hs], wide[b][:, hs], b_out_rows[:, hs],
                                          ALU.add).then_inc(s_self["y"], 1)
                    q.add("vector", at["y_copy"][b] + half, add_bias)

                def free_bank(eng, n, b=b):
                    take(eng, s_self["y"], 2)
                    pass_on(eng, s_wide_free[b])
                q.add("vector", at["y_copy"][b] + 2, free_bank)
                c = at["y_copy"][b]
                ln_stats(q, (c + 2, c + 3), c + 4, "y", y, b)

                ln_apply(q, at["y_norm"][b], "y", y, y, b, s_y_norm)

                def residual(eng, n, b=b):
                    take(eng, s_y_norm, 2)
                    if b == 0:
                        take(eng, s_x_res, 16)
                    eng.tensor_tensor(x_res[:, b, :], y[:, b, :], x_res[:, b, :], ALU.add).then_inc(s_x1, 1)
                q.add("gpsimd", at["y_norm"][b] + 1, residual)

                def arrived(eng, n, b=b):
                    take(eng, s_x1)
                c = at["r"][b]
                q.add("vector", c, arrived)
                ln_stats(q, (c, c + 1), c + 2, "r", x_res, b)

                ln_apply(q, at["r_norm"][b], "r", x1_norm, x_res, b, s_x1_norm, room=s_x1_norm_free)
                bank = 2 + b
                t2 = at["t2"][b]

                def transposes(eng, n, b=b, bank=bank):
                    take(eng, s_x1_norm, 2)
                    take(eng, s_wide_free[bank])
                    for k in range(KD):
                        ins = eng.transpose(wide[bank][:, k * P:(k + 1) * P], x1_norm[:, b, k * P:(k + 1) * P],
                                            ident[:, :])
                    ins.then_inc(s_t2, 1)
                q.add("tensor", t2, transposes)
                for half in range(2):
                    ks = slice(half * KD // 2, (half + 1) * KD // 2)

                    def high(eng, n, b=b, bank=bank, half=half, ks=ks):
                        if half == 0:
                            take(eng, s_t2)
                            pass_on(eng, s_x1_norm_free)
                            if b == batch - 1:
                                pass_on(eng, s_x_res_free)
                            if b == 0:
                                take(eng, s_x1_split_free)
                        eng.copy(x1_hi[:, ks, b * P:(b + 1) * P],
                                 wide[bank][:, half * HALF:(half + 1) * HALF].rearrange("p (k t) -> p k t", t=P)
                                 ).then_inc(s_x1_hi, 1)
                    q.add("scalar", at["t2_high"][b] + half, high)
                for half in range(2):
                    ks = slice(half * KD // 2, (half + 1) * KD // 2)

                    def low(eng, n, b=b, bank=bank, half=half, ks=ks):
                        if half == 0:
                            take(eng, s_x1_hi, 2)
                        ins = eng.tensor_tensor(
                            x1_lo[:, ks, b * P:(b + 1) * P],
                            wide[bank][:, half * HALF:(half + 1) * HALF].rearrange("p (k t) -> p k t", t=P),
                            x1_hi[:, ks, b * P:(b + 1) * P].bitcast(F32), ALU.subtract)
                        if half == 1:
                            ins.then_inc(s_x1_split, 1)
                    q.add("vector", at["t2_high"][b] + 2 + half, low)

            def keep(eng, n):
                eng.tensor_scalar(x1[:, :, :].rearrange("p b d -> p (b d)"),
                                  x_res[:, :, :].rearrange("p b d -> p (b d)"), 0.0, 1.0, ALU.add,
                                  ALU.mult).then_inc(s_pool_self, 1)
                take(eng, s_pool_self)
                pass_on(eng, s_x_res_free)
            q.add("gpsimd", at["keep"], keep)

        def tail(q, at, last=False):
            for b in range(batch):
                c = at["z_copy"][b]
                for half in range(2):
                    def rescale(eng, n, b=b, half=half):
                        hs = slice(half * HALF, (half + 1) * HALF)
                        if half == 0 and b == 0:
                            take(eng, s_out_stored, 16)
                        if half == 0:
                            take(eng, s_z_psum)
                            if b == batch - 1:
                                pass_on(eng, s_fused_split_free)
                        eng.tensor_tensor(z[:, b, hs], wide[2 + b][:, hs], down_scale_rows[:, hs],
                                          ALU.mult).then_inc(s_self["z"], 1)
                    q.add("vector", c + half, rescale)

                def free_bank(eng, n, b=b):
                    take(eng, s_self["z"], 2)
                    pass_on(eng, s_wide_free[2 + b])
                q.add("vector", c + 2, free_bank)
                ln_stats(q, at["z_halves"][b], at["z_whole"][b], "z", z, b)

                ln_apply(q, at["z_norm"][b], "z", z, z, b, s_z_norm)

                def residual(eng, n, b=b):
                    take(eng, s_z_norm, 2)
                    ins = eng.tensor_tensor(z[:, b, :], z[:, b, :], x1[:, b, :], ALU.add)
                    if b == batch - 1:
                        ins.then_inc(s_pool_self, 1)
                        take(eng, s_pool_self)
                        pass_on(eng, s_out_ready)
                q.add("gpsimd", at["z_norm"][b] + 1, residual)

            def store(eng, n):
                take(eng, s_out_ready)
                if isinstance(n, int):
                    dst = out_blocks[n - 2]
                else:
                    dst = out_blocks[bass.ds(n - 2, 1)].rearrange("o t b d -> (o t) b d")
                eng.dma_start(dst, z[:, :, :]).then_inc(s_last_stored if last else s_out_stored, 16)
            q.add("sync", at["z_norm"][-1] + 2, store)

        AT_BEFORE = {"x_halves": ((4, 5), (8, 9)), "x_whole": (10, 10), "x_norm": (16, 18), "t1": (23, 23),
                     "t1_copy": (25, 26, 27, 28), "u": (43, 50, 58, 66), "u_copy": (51, 59, 67, 74), "pairs": 75}
        AT_REST = {"next_to_last": (0, 2, 3, 5), "last": (4, 6, 7, 8), "down": 24}
        AT_AFTER = {"y": (0, 28), "y_copy": (23, 44), "y_norm": (30, 51), "r": (36, 56), "r_norm": (41, 61),
                    "t2": (57, 65), "t2_high": (57, 66), "ffn": 73, "keep": 68}
        AT_TAIL = {"z_copy": (28, 32), "z_halves": ((34, 35), (38, 39)), "z_whole": (40, 40),
                   "z_norm": (53, 64)}
        START_BEFORE = {"x_halves": ((0, 1), (4, 5)), "x_whole": (2, 6), "x_norm": (7, 9), "t1": (20, 27),
                        "t1_copy": (22, 23, 28, 29), "u": (26, 30), "u_copy": (30, 34), "pieces": 13}
        FIRST_U = {"u": (0, 1), "u_copy": (8, 16)}

        def period(n, scan, next_block, last_block, finished, load_next=None):
            q = Queue()
            if last_block:
                copy_states(q, 0, SLICES - 1)
            if scan:
                if n > 0:
                    place_u(q, 0, SLICES - 1)
                recurrence(q)
                for s in range(SLICES - 1):
                    copy_states(q, (46, 74, 97)[s], s)
            if finished and n <= NB:
                ffn_rest(q, AT_REST)
            if finished:
                tail(q, AT_TAIL, last=(n == NB + 1))
            if next_block:
                before(q, AT_BEFORE, load_next)
                for s in range(SLICES - 1):
                    place_u(q, (75, 76, 98)[s], s)
            if last_block:
                after(q, AT_AFTER, first=(n == 1))
                ffn(q, AT_AFTER, whole=not scan, first=(n == 1))
            return q

        PIECES_START, PIECES_FIRST = 5, 27
        assert PIECES_FIRST >= GATE_UP_PIECES

        start = Queue()
        setup(start)
        before(start, START_BEFORE, lambda n: 1, first=True)
        slots = iter(range(START_BEFORE["pieces"], 1000))
        for i in range(PIECES_START):
            convert(start, i, slots)
        first_period = period(0, True, True, False, False, lambda n: 2)

        first_u(start, START_BEFORE, 0)
        first_u(first_period, FIRST_U, 1)
        late_loads(first_period, range(20, T, (T - 20) // KH))
        slots = first_period.free_slots("vector", 1, T)
        for i in range(PIECES_START, PIECES_FIRST):
            convert(first_period, i, slots)

        second = period(1, True, True, True, False, lambda n: n + 2)
        second.add("vector", 0, lambda eng, n: take(eng, s_const_in, 64), rank=-3)
        slots = second.free_slots("vector", 1, T)
        guard_weights(second, slots, 0, GATE_UP_PIECES, up_q[:, KD - 1, inner - 1:inner])
        for i in range(PIECES_FIRST, NP):
            convert(second, i, slots)
        guard_weights(second, slots, GATE_UP_PIECES, NP, down_q[:, KI - 1, dim - 1:dim])
        periods = [(start, 0, 1), (first_period, 0, 1)]

        def last_weights(eng, n):
            for i in range(DOWN_IN_TIME, KI):
                take(eng, s_converted["gpsimd" if by_pool(GATE_UP_PIECES + i) else "vector"])
            take(eng, s_guarded)
        second.add("tensor", T, last_weights)
        periods.append((second, 1, 1))
        periods.append((period(2, True, True, True, True, lambda n: n + 2), 2, NB - 4))
        periods.append((period(NB - 2, True, True, True, True), NB - 2, 1))
        periods.append((period(NB - 1, True, False, True, True), NB - 1, 1))
        periods.append((period(NB, False, False, True, True), NB, 1))
        periods.append((period(NB + 1, False, False, False, True), NB + 1, 1))

        def run(name, eng):
            for q, n, turns in periods:
                if turns == 1:
                    q.emit(name, eng, n)
                else:
                    with eng.Fori(n, n + turns) as turn:
                        q.emit(name, eng, turn)

        block = ctx.enter_context(nc.Block())

        @block.sync
        def _(eng):
            for s in s_raw_free + [s_x_res_free, s_x_res_free]:
                eng.sem_inc(s, 1)
            run("sync", eng)
            eng.wait_ge(s_last_stored, 16)

        @block.tensor
        def _(eng):
            for s in s_wide_free + s_gate_up_free:
                eng.sem_inc(s, 1)
            run("tensor", eng)

        @block.vector
        def _(eng):
            for s, count in ((s_x1_norm_free, batch), (s_fused_free, NF), (s_out_stored, 16)):
                eng.sem_inc(s, count)
            run("vector", eng)

        @block.scalar
        def _(eng):
            for s, count in ((s_x_norm_t_free, 1), (s_u_rows_free, 1), (s_x1_split_free, 1),
                             (s_fused_split_free, NF),
                             (s_slice_copied, SLICES)):
                eng.sem_inc(s, count)
            run("scalar", eng)

        @block.gpsimd
        def _(eng):
            for s, count in ((s_states_free, 1),):
                eng.sem_inc(s, count)
            run("gpsimd", eng)


def kernel(**inputs):
    import numpy as _np
    import concourse.bacc as _bacc
    from concourse import mybir as _mybir
    from concourse.bass_utils import run_bass_kernel_spmd as _run

    a = {name: _np.asarray(value) for name, value in inputs.items()}

    def columns(v):
        return _np.ascontiguousarray(v.reshape(-1, P).T)

    arrays = {
        "x": a["L0_attn_x"],
        "w_in_t": a["L0_attn_W_in"].T,
        "w_out_t": a["L0_attn_W_out"].T,
        "b_in": columns(a["L0_attn_b_in"]),
        "beta": columns(a["L0_attn_beta"]),
        "gamma": columns(a["L0_attn_gamma"]),
        "b_out": a["L0_attn_b_out"].reshape(1, -1),
        "gate_w": a["L0_ffn_gate_w"],
        "up_w": a["L0_ffn_up_w"],
        "down_w": a["L0_ffn_down_w"],
        "gate_scale": columns(a["L0_ffn_gate_scale"]),
        "up_scale": columns(a["L0_ffn_up_scale"]),
        "down_scale": a["L0_ffn_down_scale"].reshape(1, -1),
        "identity": _np.eye(P, dtype=_np.float32),
    }
    arrays = {name: _np.ascontiguousarray(value) for name, value in arrays.items()}
    nc = _bacc.Bacc("TRN2", target_bir_lowering=False, num_devices=1)
    args = [nc.dram_tensor(name, v.shape, _mybir.dt.from_np(v.dtype), kind="ExternalInput").ap()
            for name, v in arrays.items()]
    shape = a["L0_attn_x"].shape
    args.append(nc.dram_tensor("out", shape, _mybir.dt.float32, kind="ExternalOutput").ap())
    recurrent_sandwich_kernel(nc, *args)
    r = _run(nc, [arrays], core_ids=[0])
    return r.results[0]["out"]
```

```python
from contextlib import ExitStack

import concourse.bass as bass
from concourse import mybir

P = 128
F32 = mybir.dt.float32
F32R = mybir.dt.float32r
I32 = mybir.dt.int32
ALU = mybir.AluOpType
ACT = mybir.ActivationFunctionType
AX_X = mybir.AxisListType.X
LN_EPS = 1e-5

EXPONENT_BITS = 0x7F800000
LEAST_NORMAL = 2.0 ** -6
ROUNDING_CONSTANT = 1.5 * 2.0 ** 20
E4M3FN_OVERFLOW = 464.0
HUGE = 1e38


class Queue:

    def __init__(self):
        self.items = {"sync": [], "tensor": [], "vector": [], "scalar": [], "gpsimd": []}
        self.added = 0

    def add(self, engine, slot, emit, rank=1):
        self.added += 1
        self.items[engine].append((slot, rank, self.added, emit))

    def free_slots(self, engine, first, end):
        used = {int(slot) for slot, rank, _, _ in self.items[engine] if rank == 1}
        return iter([slot for slot in range(first, end) if slot not in used])

    def emit(self, engine, eng, n):
        for _, _, _, emit in sorted(self.items[engine], key=lambda item: item[:3]):
            emit(eng, n)
        take_out(eng)


TAKEN = {}


def take(eng, sem, count=1):
    seen = TAKEN.get(sem.name, (0, sem))[0] + count
    TAKEN[sem.name] = (seen, sem)
    eng.wait_ge(sem, seen)


def take_out_one(eng):
    if TAKEN:
        seen, sem = TAKEN.pop(next(iter(TAKEN)))
        eng.sem_inc(sem, -seen)


def take_out(eng):
    while TAKEN:
        take_out_one(eng)


def pass_on(eng, sem):
    eng.sem_inc(sem, 1)


def recurrent_sandwich_kernel(nc, x, w_in_t, w_out_t, b_in, beta, gamma, b_out, gate_w, up_w, down_w,
                              gate_scale, up_scale, down_scale, identity, out):
    batch, seq, dim = x.shape
    hidden = w_in_t.shape[1]
    inner = gate_w.shape[1]
    KD = dim // P
    KH = hidden // P
    KI = inner // P
    T = 128
    NB = seq // T
    CH = KH * batch
    TOK = batch * T
    SLICES = 4
    TS = T // SLICES
    HALF = dim // 2
    GROUPS = batch
    TH = T // GROUPS
    QUADS = KH // 4
    assert T == P and TOK == 256 and dim == 512 and seq % T == 0

    x_blocks = x.rearrange("b (n t) d -> n t b d", t=T)
    out_blocks = out.rearrange("b (n t) d -> n t b d", t=T)

    with ExitStack() as ctx:
        def sb(name, shape, dt=F32):
            return ctx.enter_context(nc.sbuf_tensor(name, shape, dt))

        def ps(name, shape):
            return ctx.enter_context(nc.psum_tensor(name, shape, F32))

        def sem(name):
            return ctx.enter_context(nc.semaphore(name))

        w_in_sb = sb("w_in_sb", [P, KD, hidden])
        w_out_sb = sb("w_out_sb", [P, KH, dim])
        gate_q = sb("gate_q", [P, KD, inner], F32R)
        up_q = sb("up_q", [P, KD, inner], F32R)
        down_q = sb("down_q", [P, KI, dim], F32R)
        ident = sb("ident", [P, P])
        b_out_rows = sb("b_out_rows", [P, dim])
        down_scale_rows = sb("down_scale_rows", [P, dim])
        cols = sb("cols", [P, 3, KH])
        u_bias = sb("u_bias", [P, KH])
        gate_scale_cols = sb("gate_scale_cols", [P, KI])
        up_scale_sb = sb("up_scale_sb", [P, KI])
        minus_half = sb("minus_half", [P, 2])
        warm = sb("warm", [P, 2])
        factors = sb("factors", [P, CH, 2])

        OWN = 3
        raw_own = sb("raw_own", [P, OWN, dim])
        rounder_own = sb("rounder_own", [P, OWN, dim])
        pieces = []
        for k in range(KD):
            for w_dram, w_q in ((gate_w, gate_q), (up_w, up_q)):
                for c in range(inner // dim):
                    pieces.append((w_dram[k * P:(k + 1) * P, c * dim:(c + 1) * dim],
                                   w_q[:, k, c * dim:(c + 1) * dim]))
        for i in range(KI):
            pieces.append((down_w[i * P:(i + 1) * P, :], down_q[:, i, :]))
        NP = len(pieces)
        peaks = sb("peaks", [P, NP, 2])
        guard = sb("guard", [P, 3])

        x_in = sb("x_in", [P, batch, dim])
        x_norm_t = sb("x_norm_t", [P, KD, TOK])
        u_rows = sb("u_rows", [P, CH, T])
        pairs = sb("pairs", [P, T, CH, 2])
        states = sb("states", [P, CH, T])
        states_by_time = states[:, :, :].rearrange("p c t -> p (c t)").rearrange(
            "p (j g b t) -> p j g b t", j=KH, g=GROUPS, b=batch)
        x_res = sb("x_res", [P, batch, dim])
        y = sb("y", [P, batch, dim])
        x1 = sb("x1", [P, batch, dim])
        x1_norm = sb("x1_norm", [P, batch, dim])
        x1_hi = sb("x1_hi", [P, KD, TOK], F32R)
        x1_lo = sb("x1_lo", [P, KD, TOK], F32R)
        NF = 3
        sigm = sb("sigm", [P, NF, TOK])
        gated = sb("gated", [P, NF, TOK])
        fused = sb("fused", [P, NF, TOK])
        fused_hi = sb("fused_hi", [P, NF, TOK], F32R)
        fused_lo = sb("fused_lo", [P, NF, TOK], F32R)
        z = sb("z", [P, batch, dim])
        RAW = OWN + 1
        raw = [raw_own[:, r, :] for r in range(OWN)] + [z[:, 0, :]]
        rounder = [rounder_own[:, r, :] for r in range(OWN)] + [z[:, 1, :]]
        stats = {w: sb(f"stats_{w}", [P, batch, 2, nc.vector.BN_STATS_DIM]) for w in "xyrz"}
        mean_var = {w: sb(f"mean_var_{w}", [P, batch, nc.vector.BN_AGGR_DIM]) for w in "xyrz"}
        var_eps = {w: sb(f"var_eps_{w}", [P, batch]) for w in "xyrz"}
        rstd = {w: sb(f"rstd_{w}", [P, batch]) for w in "xyrz"}

        preact = ps("preact", [P, 2, CH, 2])
        wide = [ps(f"wide{i}", [P, 512]) for i in range(4)]
        NG = 3
        gate_up = [ps(f"gate_up{i}", [P, 2, TOK]) for i in range(NG)]

        s_const_in = sem("s_const_in")
        s_small_in = sem("s_small_in")
        s_w_in_in = [sem(f"s_w_in_in{m}") for m in range(KH // 2)]
        s_w_out_in = sem("s_w_out_in")
        s_ident_in = sem("s_ident_in")
        s_raw_in = [sem(f"s_raw_in{i}") for i in range(RAW)]
        s_raw_free = [sem(f"s_raw_free{i}") for i in range(RAW)]
        s_piece_ready = sem("s_piece_ready")
        s_converted = {who: sem(f"s_converted_by_{who}") for who in ("gpsimd", "vector")}
        s_pool_self = sem("s_pool_self")
        s_self = {w: sem(f"s_self_{w}") for w in ("x", "y", "r", "z", "fused", "pieces", "rounding", "setup")}
        s_scalar_self = sem("s_scalar_self")
        s_warm = sem("s_warm")
        s_setup = sem("s_setup")
        s_bias_ready = sem("s_bias_ready")
        s_guarded = sem("s_guarded")
        s_x_in = sem("s_x_in")
        s_x_in_free = sem("s_x_in_free")
        s_mv = {w: sem(f"s_mv_{w}") for w in "xyrz"}
        s_rstd = {w: sem(f"s_rstd_{w}") for w in "xyrz"}
        s_x_norm = sem("s_x_norm")
        s_t1 = sem("s_t1")
        s_x_norm_t = sem("s_x_norm_t")
        s_x_norm_t_free = sem("s_x_norm_t_free")
        s_u_psum = sem("s_u_psum")
        s_u_rows = sem("s_u_rows")
        s_u_rows_free = sem("s_u_rows_free")
        s_pairs_u = sem("s_pairs_u")
        s_preact = sem("s_preact")
        s_state = sem("s_state")
        s_slice_done = sem("s_slice_done")
        s_slice_copied = sem("s_slice_copied")
        s_states = sem("s_states")
        s_states_free = sem("s_states_free")
        s_wide_free = [sem(f"s_wide_free{i}") for i in range(4)]
        s_gate_up_free = [sem(f"s_gate_up_free{i}") for i in range(NG)]
        s_y_psum = sem("s_y_psum")
        s_x_res = sem("s_x_res")
        s_x_res_free = sem("s_x_res_free")
        s_y_norm = sem("s_y_norm")
        s_x1 = sem("s_x1")
        s_x1_norm = sem("s_x1_norm")
        s_x1_norm_free = sem("s_x1_norm_free")
        s_t2 = sem("s_t2")
        s_x1_hi = sem("s_x1_hi")
        s_x1_split = sem("s_x1_split")
        s_x1_split_free = sem("s_x1_split_free")
        s_gate_up = sem("s_gate_up")
        s_sigm = sem("s_sigm")
        s_fused = sem("s_fused")
        s_fused_hi = sem("s_fused_hi")
        s_fused_free = sem("s_fused_free")
        s_fused_split = sem("s_fused_split")
        s_fused_split_free = sem("s_fused_split_free")
        s_z_psum = sem("s_z_psum")
        s_z_norm = sem("s_z_norm")
        s_z_norm_self = sem("s_z_norm_self")
        s_last_ready = sem("s_last_ready")
        s_out_ready = sem("s_out_ready")
        s_out_stored = sem("s_out_stored")
        s_last_stored = sem("s_last_stored")

        def ln_stats(q, halves_at, whole_at, w, src, b):
            for half in range(2):
                def halves(eng, n, half=half):
                    eng.bn_stats(stats[w][:, b, half, :], src[:, b, half * HALF:(half + 1) * HALF]).then_inc(
                        s_self[w], 1)
                q.add("vector", halves_at[half], halves)

            def aggregate(eng, n):
                take(eng, s_self[w], 2)
                eng.bn_aggr(mean_var[w][:, b, :], stats[w][:, b, :, :].rearrange("p h s -> p (h s)")).then_inc(
                    s_mv[w], 1)
            q.add("vector", whole_at, aggregate)

            def root(eng, n):
                take(eng, s_mv[w])
                eng.tensor_scalar(var_eps[w][:, b:b + 1], mean_var[w][:, b, 1:2], LN_EPS, 1.0, ALU.add,
                                  ALU.mult).then_inc(s_pool_self, 1)
                take(eng, s_pool_self)
                eng.tensor_tensor(rstd[w][:, b:b + 1], var_eps[w][:, b:b + 1], minus_half[:, 0:1],
                                  ALU.pow).then_inc(s_rstd[w], 1)
            q.add("gpsimd", whole_at, root)

        def ln_apply(q, slot, w, dst, src, b, done, room=None):
            for half in range(2):
                def norm(eng, n, half=half, hs=slice(half * HALF, (half + 1) * HALF)):
                    if half == 0:
                        take(eng, s_rstd[w])
                        if room is not None:
                            take(eng, room)
                    eng.tensor_scalar(dst[:, b, hs], src[:, b, hs], mean_var[w][:, b, 0:1], rstd[w][:, b:b + 1],
                                      ALU.subtract, ALU.mult).then_inc(done, 1)
                q.add("vector", slot + half, norm)

        def setup(q):
            def loads(eng, n):
                for b in range(batch):
                    eng.dma_start(x_in[b * TH:(b + 1) * TH, :, :],
                                  x_blocks[0][:, b, :].rearrange("(g t) d -> t g d", g=GROUPS)).then_inc(s_x_in, 16)
                eng.dma_start(ident[:, :], identity).then_inc(s_ident_in, 16)
                eng.dma_start(cols[:, 0, :], b_in).then_inc(s_small_in, 16)
                eng.dma_start(cols[:, 1, :], beta).then_inc(s_small_in, 16)
                eng.dma_start(cols[:, 2, :], gamma).then_inc(s_small_in, 16)
                eng.dma_start(gate_scale_cols[:, :], gate_scale).then_inc(s_const_in, 16)
                eng.dma_start(up_scale_sb[:, :], up_scale).then_inc(s_const_in, 16)
            q.add("sync", 0, loads)

            for m in range(KH // 2):
                def load_w_in(eng, n, m=m, ms=slice(2 * m * P, 2 * (m + 1) * P)):
                    eng.dma_start(w_in_sb[:, :, ms], w_in_t[:, ms].rearrange("(k p) h -> p k h", p=P)
                                  ).then_inc(s_w_in_in[m], 16)
                q.add("sync", START_BEFORE["w_in"][m], load_w_in)

            def first_vector(eng, n):
                eng.memset(warm[:, :], 0.0).then_inc(s_warm, 1)
                eng.memset(factors[:, :, :], 0.0).then_inc(s_self["setup"], 1)
                eng.memset(pairs[:, 0, :, :], 0.0).then_inc(s_self["setup"], 1)
                take(eng, s_self["setup"], 2)
                pass_on(eng, s_setup)
            q.add("vector", 0, first_vector)

            def first_pool(eng, n):
                eng.memset(minus_half[:, :], -0.5).then_inc(s_pool_self, 1)
                take(eng, s_pool_self)
                take(eng, s_setup)
            q.add("gpsimd", 0, first_pool)

            def small_vector(eng, n):
                take(eng, s_small_in, 48)
                eng.tensor_tensor(u_bias[:, :], cols[:, 0, :], cols[:, 1, :], ALU.add).then_inc(s_self["setup"], 1)
                for b in range(batch):
                    eng.tensor_copy(factors[:, b:CH:batch, 1], cols[:, 2, :]).then_inc(s_self["setup"], 1)
                take(eng, s_self["setup"], 1 + batch)
                pass_on(eng, s_bias_ready)
            q.add("vector", 3, small_vector)

            def warm_up(eng, n):
                take(eng, s_warm)
                eng.activation(warm[:, 0:1], warm[:, 1:2], ACT.Sigmoid)
                take(eng, s_bias_ready)
            q.add("scalar", 0, warm_up)

        def late_loads(q, slots):
            def rows(eng, n):
                eng.dma_start(b_out_rows[:, :], b_out.to_broadcast([P, dim])).then_inc(s_const_in, 16)
                eng.dma_start(down_scale_rows[:, :], down_scale.to_broadcast([P, dim])).then_inc(s_const_in, 16)
            q.add("sync", slots[0], rows)
            for j in range(KH):
                def load(eng, n, j=j):
                    eng.dma_start(w_out_sb[:, j, :], w_out_t[j * P:(j + 1) * P, :]).then_inc(s_w_out_in, 16)
                q.add("sync", slots[j], load)

        GATE_UP_PIECES = NP - KI

        def by_pool(i):
            return i % 4 != 3 if i < GATE_UP_PIECES else i % 3 != 2

        LAST_POOL_GATE_UP = max(i for i in range(GATE_UP_PIECES) if by_pool(i))
        assert not by_pool(GATE_UP_PIECES - 1) and not by_pool(NP - 1)

        LOAD_AHEAD = 10
        room_at = {}

        def convert(q, i, slots):
            src, dst = pieces[i]
            r = i % RAW
            on_pool = by_pool(i)
            slot = next(slots)

            def load(eng, n):
                take(eng, s_raw_free[r])
                eng.dma_start(raw[r], src).then_inc(s_raw_in[r], 16)
            room_q, room_slot = room_at.get(i - RAW, (q, 0))
            q.add("sync", max(slot - LOAD_AHEAD, room_slot if room_q is q else -LOAD_AHEAD), load)

            def binade(eng, n):
                take(eng, s_raw_in[r], 16)
                eng.tensor_scalar(rounder[r].bitcast(I32), raw[r].bitcast(I32), EXPONENT_BITS, None,
                                  ALU.bitwise_and).then_inc(s_self["pieces"], 1)
            q.add("vector", slot, binade)

            for half in range(2):
                def peak(eng, n, hs=slice(half * HALF, (half + 1) * HALF), half=half):
                    eng.tensor_reduce(peaks[:, i, half:half + 1], raw[r][:, hs], AX_X, ALU.max,
                                      apply_absolute_value=True).then_inc(s_self["pieces"], 1)
                q.add("vector", next(slots), peak)

            def constant(eng, n):
                take(eng, s_self["pieces"], 3)
                eng.tensor_scalar(rounder[r], rounder[r], LEAST_NORMAL, ROUNDING_CONSTANT, ALU.max,
                                  ALU.mult).then_inc(s_piece_ready if on_pool else s_self["rounding"], 1)
            slot = next(slots)
            q.add("vector", slot, constant)

            who, me = ("gpsimd", s_pool_self) if on_pool else ("vector", s_self["rounding"])
            parts = 1 if on_pool else 2
            size = dim // parts
            for part in range(parts):
                def add_constant(eng, n, part=part, cs=slice(part * size, (part + 1) * size)):
                    if part == 0:
                        take(eng, s_piece_ready if on_pool else me)
                    eng.tensor_tensor(raw[r][:, cs], raw[r][:, cs], rounder[r][:, cs], ALU.add).then_inc(me, 1)
                q.add(who, slot if on_pool else next(slots), add_constant)
            for part in range(parts):
                def take_off(eng, n, part=part, cs=slice(part * size, (part + 1) * size)):
                    if part == 0:
                        take(eng, me, parts)
                    eng.tensor_tensor(dst[:, cs], raw[r][:, cs], rounder[r][:, cs], ALU.subtract).then_inc(me, 1)
                slot = slot if on_pool else next(slots)
                q.add(who, slot, take_off)

            def report(eng, n):
                take(eng, me, parts)
                if i < NP - RAW:
                    pass_on(eng, s_raw_free[r])
                if i == LAST_POOL_GATE_UP or i >= GATE_UP_PIECES:
                    pass_on(eng, s_converted[who])
            slot = slot if on_pool else next(slots)
            room_at[i] = (q, slot)
            q.add(who, slot, report)

        def guard_weights(q, slots, first, end, poisoned):
            steps = (
                lambda eng: eng.tensor_reduce(guard[:, 0:1], peaks[:, first:end, :].rearrange("p i h -> p (i h)"),
                                              AX_X, ALU.max),
                lambda eng: eng.tensor_scalar(guard[:, 1:2], guard[:, 0:1], E4M3FN_OVERFLOW, E4M3FN_OVERFLOW,
                                              ALU.max, ALU.subtract),
                lambda eng: eng.tensor_scalar(guard[:, 2:3], guard[:, 1:2], HUGE, HUGE, ALU.mult, ALU.mult),
                lambda eng: eng.scalar_tensor_tensor(out=poisoned, in0=guard[:, 2:3], scalar=0.0,
                                                     in1=poisoned.bitcast(F32), op0=ALU.mult, op1=ALU.add),
            )
            for i, step in enumerate(steps):
                def run_step(eng, n, i=i, step=step):
                    if i:
                        take(eng, s_self["setup"])
                    step(eng).then_inc(s_self["setup"], 1)
                q.add("vector", next(slots), run_step)

            def report(eng, n):
                take(eng, s_self["setup"])
                pass_on(eng, s_guarded)
            q.add("vector", next(slots), report)

        def before(q, at, load_next, first=False):
            for b in range(batch):
                if b == 0:
                    def arrived(eng, n):
                        take(eng, s_x_in, 16 * batch if first else 16)
                    q.add("vector", at["x_halves"][0][0], arrived)
                ln_stats(q, at["x_halves"][b], at["x_whole"][b], "x", x_in, b)
            for b in range(batch):
                ln_apply(q, at["x_norm"][b], "x", x_in, x_in, b, s_x_norm)
            if load_next is not None:
                def load(eng, n):
                    take(eng, s_x_in_free)
                    if isinstance(n, int):
                        src = x_blocks[load_next(n)]
                    else:
                        src = x_blocks[bass.ds(load_next(n), 1)].rearrange("o t b d -> (o t) b d")
                    eng.dma_start(x_in[:, :, :], src).then_inc(s_x_in, 16)
                q.add("sync", at["t1_copy"][-1], load)
            for b in range(batch):
                bank = gate_up[b][:, :, :].rearrange("p v t -> p (v t)")

                def transposes(eng, n, b=b, bank=bank):
                    if first and b == 0:
                        take(eng, s_ident_in, 16)
                    take(eng, s_x_norm, 2)
                    take(eng, s_gate_up_free[b])
                    for k in range(KD):
                        ins = eng.transpose(bank[:, k * P:(k + 1) * P], x_in[:, b, k * P:(k + 1) * P],
                                            ident[:, :])
                    ins.then_inc(s_t1, 1)
                q.add("tensor", at["t1"][b], transposes)
                for half in range(2):
                    def copy(eng, n, b=b, bank=bank, half=half):
                        if half == 0:
                            take(eng, s_t1)
                            if b == 0 and not first:
                                take(eng, s_x_norm_t_free)
                            if b == batch - 1:
                                pass_on(eng, s_x_in_free)
                        ks = slice(half * KD // 2, (half + 1) * KD // 2)
                        ins = eng.copy(x_norm_t[:, ks, b * P:(b + 1) * P],
                                       bank[:, half * HALF:(half + 1) * HALF].rearrange("p (k t) -> p k t", t=P))
                        if half == 1:
                            ins.then_inc(s_x_norm_t, 1)
                    q.add("scalar", at["t1_copy"][2 * b + half], copy)
            if first:
                return
            for m in range(KH // 2):
                bank = m % 2

                def project(eng, n, m=m, bank=bank):
                    if m == 0:
                        take(eng, s_x_norm_t, batch)
                        for b in range(batch):
                            pass_on(eng, s_gate_up_free[b])
                    take(eng, s_wide_free[bank])
                    for jj in range(2):
                        j = 2 * m + jj
                        for k in range(KD):
                            ins = eng.matmul(wide[bank][:, jj * TOK:(jj + 1) * TOK],
                                             w_in_sb[:, k, j * P:(j + 1) * P], x_norm_t[:, k, :],
                                             start=(k == 0), stop=(k == KD - 1))
                    ins.then_inc(s_u_psum, 1)
                q.add("tensor", at["u"][m], project)
                for jj in range(2):
                    def add_bias(eng, n, m=m, bank=bank, jj=jj):
                        j = 2 * m + jj
                        if jj == 0:
                            take(eng, s_u_psum)
                            if m == 0:
                                take(eng, s_u_rows_free)
                            if m == KH // 2 - 1:
                                pass_on(eng, s_x_norm_t_free)
                        chains = slice(j * batch, (j + 1) * batch)
                        ins = eng.activation(u_rows[:, chains, :].rearrange("p b t -> p (b t)"),
                                             wide[bank][:, jj * TOK:(jj + 1) * TOK], ACT.Identity,
                                             bias=u_bias[:, j:j + 1])
                        if jj == 1:
                            ins.then_inc(s_wide_free[bank] if m < KH // 2 - 1 else s_u_rows, 1)
                    q.add("scalar", at["u_copy"][m] + jj, add_bias)

            def relay_u(eng, n):
                take(eng, s_u_rows)
                pass_on(eng, s_wide_free[(KH // 2 - 1) % 2])
            q.add("gpsimd", at["pairs"], relay_u)

        def first_u(q, at, g):
            for quad in range(QUADS):
                bank = quad % 2

                def project(eng, n, quad=quad, bank=bank):
                    if quad == 0:
                        take(eng, s_x_norm_t)
                        pass_on(eng, s_gate_up_free[g])
                    take(eng, s_wide_free[bank])
                    for jj in range(4):
                        j = 4 * quad + jj
                        if g == 0 and jj % 2 == 0:
                            take(eng, s_w_in_in[j // 2], 16)
                        for k in range(KD):
                            ins = eng.matmul(wide[bank][:, jj * P:(jj + 1) * P], w_in_sb[:, k, j * P:(j + 1) * P],
                                             x_norm_t[:, k, g * P:(g + 1) * P], start=(k == 0), stop=(k == KD - 1))
                    ins.then_inc(s_u_psum, 1)
                q.add("tensor", at["u"][quad], project)
                for jj in range(4):
                    def add_bias(eng, n, quad=quad, bank=bank, jj=jj):
                        j = 4 * quad + jj
                        if jj == 0:
                            take(eng, s_u_psum)
                        ins = eng.activation(
                            pairs[:, g * TH:(g + 1) * TH, j * batch:(j + 1) * batch, 1].rearrange("p t b -> p b t"),
                            wide[bank][:, jj * P:(jj + 1) * P].rearrange("p (b t) -> p b t", b=batch),
                            ACT.Identity, bias=u_bias[:, j:j + 1])
                        if jj == 3:
                            ins.then_inc(s_scalar_self, 1)
                            take(eng, s_scalar_self)
                            pass_on(eng, s_wide_free[bank])
                            if quad == QUADS - 1:
                                eng.sem_inc(s_pairs_u, SLICES // GROUPS)
                    q.add("scalar", at["u_copy"][quad] + jj, add_bias)

        def place_u(q, slot, s):
            def place(eng, n):
                ts = slice(s * TS, (s + 1) * TS)
                ins = eng.tensor_scalar(pairs[:, ts, :, 1].rearrange("p t c -> p c t"), u_rows[:, :, ts], 0.0, 1.0,
                                          ALU.add, ALU.mult)
                if s < SLICES - 1:
                    ins.then_inc(s_pairs_u, 1)
                else:
                    ins.then_inc(s_pool_self, 1)
                    take(eng, s_pool_self)
                    pass_on(eng, s_pairs_u)
                    pass_on(eng, s_u_rows_free)
            q.add("gpsimd", slot, place)

        def recurrence(q):
            for t in range(T):
                def pre_activation(eng, n, t=t):
                    if t:
                        take(eng, s_state)
                    else:
                        take(eng, s_pairs_u)
                    eng.tensor_tensor_scan(preact[:, t % 2, :, :].rearrange("p c k -> p (c k)"),
                                           factors[:, :, :].rearrange("p c k -> p (c k)"),
                                           pairs[:, t, :, :].rearrange("p c k -> p (c k)"), 0.0, ALU.mult,
                                           ALU.add).then_inc(s_preact, 1)
                    if t and t % TS == 0:
                        pass_on(eng, s_slice_done)
                    if t + 1 < T and (t + 1) % TS == 0:
                        take(eng, s_pairs_u)
                    take_out_one(eng)
                q.add("vector", t, pre_activation, rank=-2)

                def state(eng, n, t=t):
                    if t == 0:
                        take(eng, s_slice_copied)
                    take(eng, s_preact)
                    eng.activation(pairs[:, (t + 1) % T, :, 0], preact[:, t % 2, :, 1], ACT.Tanh).then_inc(s_state, 1)
                    if t + 1 < T and (t + 1) % TS == 0:
                        take(eng, s_slice_copied)
                    take_out_one(eng)
                q.add("scalar", t, state, rank=-1)

            def end_vector(eng, n):
                take(eng, s_state)
                pass_on(eng, s_slice_done)
            q.add("vector", T, end_vector, rank=2)

        def copy_states(q, slot, s, tell=False, by_time=False):
            def collect(eng, n):
                take(eng, s_slice_done)
                if s == 0:
                    take(eng, s_states_free)

                def rows(begin, end):
                    if not by_time:
                        return states[:, :, begin:end]
                    g = begin // TH
                    return states_by_time[:, :, g, :, begin - g * TH:end - g * TH]

                def of_pairs(begin, end):
                    if not by_time:
                        return pairs[:, begin:end, :, 0].rearrange("p t c -> p c t")
                    return pairs[:, begin:end, :, 0].rearrange("p t (j b) -> p j b t", b=batch)
                first, last = s * TS + 1, (s + 1) * TS + 1
                end = min(last, T)
                ins = eng.tensor_scalar(rows(first - 1, end - 1), of_pairs(first, end), 0.0, 1.0, ALU.add, ALU.mult)
                if last > T:
                    ins = eng.tensor_scalar(rows(T - 1, T), of_pairs(0, 1), 0.0, 1.0, ALU.add, ALU.mult)
                if tell:
                    ins.then_inc(s_pool_self, 1)
                    take(eng, s_pool_self)
                    pass_on(eng, s_states)
                    pass_on(eng, s_slice_copied)
                else:
                    ins.then_inc(s_slice_copied, 1)
            q.add("gpsimd", slot, collect)

        LAG = 3
        GATE_UP_SLOTS = 3.75
        DOWN_SLOTS = 1.87

        def down_chunk(q, i, slot, first=False):
            f = i % NF

            def products(eng, n):
                take(eng, s_fused_split)
                if first:
                    take(eng, s_converted["gpsimd" if by_pool(GATE_UP_PIECES + i) else "vector"])
                for b in range(batch):
                    if i == 0:
                        take(eng, s_wide_free[2 + b])
                    for part in (fused_hi, fused_lo):
                        ins = eng.matmul(wide[2 + b][:, :], part[:, f, b * P:(b + 1) * P], down_q[:, i, :],
                                         start=(i == 0 and part is fused_hi),
                                         stop=(i == KI - 1 and part is fused_lo))
                    if i == KI - 1:
                        ins.then_inc(s_z_psum, 1)
                if i < KI - 1:
                    ins.then_inc(s_fused_split_free, 1)
            q.add("tensor", slot, products)

        def gate_up_products(q, i, slot, first=False, by_time=False):
            g = i % NG

            def products(eng, n):
                if i == 0:
                    take(eng, s_x1_split, batch)
                    for b in range(batch):
                        pass_on(eng, s_wide_free[b if by_time else 2 + b])
                    if first:
                        take(eng, s_guarded)
                        take(eng, s_converted["gpsimd"])
                take(eng, s_gate_up_free[g])
                for v, w_q in enumerate((gate_q, up_q)):
                    for k in range(KD):
                        for part in (x1_hi, x1_lo):
                            ins = eng.matmul(gate_up[g][:, v, :], w_q[:, k, i * P:(i + 1) * P], part[:, k, :],
                                             start=(k == 0 and part is x1_hi),
                                             stop=(k == KD - 1 and part is x1_lo))
                ins.then_inc(s_gate_up, 1)
            q.add("tensor", slot, products)

        def gate_up_use(q, i, sigmoid_at, silu_at, up_at, high_at):
            g = i % NG
            f = i % NF

            def sigmoid(eng, n):
                take(eng, s_gate_up)
                if i == KI - 1:
                    pass_on(eng, s_x1_split_free)
                eng.activation(sigm[:, f, :], gate_up[g][:, 0, :], ACT.Sigmoid,
                               scale=gate_scale_cols[:, i:i + 1]).then_inc(s_sigm, 1)
            q.add("scalar", sigmoid_at, sigmoid)

            def silu(eng, n):
                take(eng, s_sigm)
                eng.scalar_tensor_tensor(out=gated[:, f, :], in0=gate_up[g][:, 0, :],
                                         scalar=gate_scale_cols[:, i:i + 1], in1=sigm[:, f, :], op0=ALU.mult,
                                         op1=ALU.mult).then_inc(s_self["fused"], 1)
            q.add("vector", silu_at, silu)

            def times_up(eng, n):
                take(eng, s_self["fused"])
                take(eng, s_fused_free)
                eng.scalar_tensor_tensor(out=fused[:, f, :], in0=gate_up[g][:, 1, :],
                                         scalar=up_scale_sb[:, i:i + 1], in1=gated[:, f, :], op0=ALU.mult,
                                         op1=ALU.mult).then_inc(s_fused, 1)
            q.add("vector", up_at, times_up)

            def release(eng, n):
                take(eng, s_fused)
                pass_on(eng, s_gate_up_free[g])
            q.add("scalar", min(up_at + 1, high_at), release, rank=0)

            def high(eng, n):
                take(eng, s_fused_split_free)
                eng.copy(fused_hi[:, f, :], fused[:, f, :]).then_inc(s_fused_hi, 1)
            q.add("scalar", high_at, high)

            def low(eng, n):
                take(eng, s_fused_hi)
                eng.tensor_tensor(fused_lo[:, f, :], fused[:, f, :], fused_hi[:, f, :].bitcast(F32),
                                  ALU.subtract).then_inc(s_pool_self, 1)
                take(eng, s_pool_self)
                pass_on(eng, s_fused_free)
                pass_on(eng, s_fused_split)
            q.add("gpsimd", high_at, low)

        CHUNKS_IN_TIME = KI - 1
        DOWN_IN_TIME = CHUNKS_IN_TIME - LAG

        def ffn_chunks(q, at, begin, end, used, first=False, by_time=False, beside=True):
            for i in range(begin, end):
                slot = at + GATE_UP_SLOTS * (i - begin) + DOWN_SLOTS * max(0, i - max(begin, LAG))
                gate_up_products(q, i, slot, first, by_time)
                if i >= LAG:
                    down_chunk(q, i - LAG, slot + GATE_UP_SLOTS, first)
                if i < used:
                    if beside:
                        c = int(slot + 4.7)
                        gate_up_use(q, i, c, c + 2, c + 3, c + (5 if i < LAG else 4))
                    else:
                        c = slot + GATE_UP_SLOTS
                        gate_up_use(q, i, c, c + 1.2, c + 1.4, c + 2.4)
            if end == KI:
                for i in range(KI - LAG, KI):
                    down_chunk(q, i, slot + 6)

        def ffn_rest(q, at):
            gate_up_products(q, KI - 1, -2)
            gate_up_use(q, KI - 2, *at["next_to_last"])
            gate_up_use(q, KI - 1, *at["last"])
            for i in range(DOWN_IN_TIME, KI):
                down_chunk(q, i, -1 if i < KI - 2 else at["down"])

        def project_y(q, slot, b, first=False, by_time=False):
            def project(eng, n):
                if first and b == 0:
                    take(eng, s_w_out_in, 16 * KH)
                if b == 0 or by_time:
                    take(eng, s_states)
                take(eng, s_wide_free[b])
                for j in range(KH):
                    if by_time:
                        rows = states_by_time[:, j, b, :, :].rearrange("p b t -> p (b t)")
                    else:
                        rows = states[:, j * batch + b, :]
                    ins = eng.matmul(wide[b][:, :], rows, w_out_sb[:, j, :], start=(j == 0), stop=(j == KH - 1))
                ins.then_inc(s_y_psum, 1)
            q.add("tensor", slot, project)

        def load_last_residual(q, slot):
            def load(eng, n):
                take(eng, s_x_res_free, 2)
                for b in range(batch):
                    eng.dma_start(x_res[b * TH:(b + 1) * TH, :, :],
                                  x_blocks[NB - 1][:, b, :].rearrange("(g t) d -> t g d", g=GROUPS)
                                  ).then_inc(s_x_res, 16)
            q.add("sync", slot, load)

        def load_residual(q):
            def load(eng, n):
                take(eng, s_x_res_free, 2)
                if isinstance(n, int):
                    src = x_blocks[n - 1]
                else:
                    src = x_blocks[bass.ds(n - 1, 1)].rearrange("o t b d -> (o t) b d")
                eng.dma_start(x_res[:, :, :], src).then_inc(s_x_res, 16)
            q.add("sync", 0, load)

        def norms(q, at, b, by_time=False):
            for half in range(2):
                def add_bias(eng, n, b=b, half=half):
                    hs = slice(half * HALF, (half + 1) * HALF)
                    if half == 0:
                        take(eng, s_y_psum)
                        if b == batch - 1:
                            pass_on(eng, s_states_free)
                    eng.tensor_tensor(y[:, b, hs], wide[b][:, hs], b_out_rows[:, hs],
                                      ALU.add).then_inc(s_self["y"], 1)
                q.add("vector", at["y_copy"][b] + half, add_bias)

            def free_bank(eng, n, b=b):
                take(eng, s_self["y"], 2)
                pass_on(eng, s_wide_free[b])
            q.add("vector", at["y_copy"][b] + 2, free_bank)
            c = at["y_copy"][b]
            ln_stats(q, (c + 2, c + 3), c + 4, "y", y, b)

            ln_apply(q, at["y_norm"][b], "y", y, y, b, s_y_norm)

            def residual(eng, n, b=b):
                take(eng, s_y_norm, 2)
                if b == 0:
                    take(eng, s_x_res, 16 * batch if by_time else 16)
                eng.tensor_tensor(x_res[:, b, :], y[:, b, :], x_res[:, b, :], ALU.add).then_inc(s_x1, 1)
            q.add("gpsimd", at["y_norm"][b] + 1, residual)

            def arrived(eng, n, b=b):
                take(eng, s_x1)
            c = at["r"][b]
            q.add("vector", c, arrived)
            ln_stats(q, (c, c + 1), c + 2, "r", x_res, b)

            ln_apply(q, at["r_norm"][b], "r", x1_norm, x_res, b, s_x1_norm, room=s_x1_norm_free)

        def transpose_and_split(q, at, b, by_time=False):
            bank = b if by_time else 2 + b
            t2 = at["t2"][b]

            def transposes(eng, n, b=b, bank=bank):
                take(eng, s_x1_norm, 2)
                take(eng, s_wide_free[bank])
                for k in range(KD):
                    ins = eng.transpose(wide[bank][:, k * P:(k + 1) * P], x1_norm[:, b, k * P:(k + 1) * P],
                                        ident[:, :])
                ins.then_inc(s_t2, 1)
            q.add("tensor", t2, transposes)
            for half in range(2):
                ks = slice(half * KD // 2, (half + 1) * KD // 2)

                def high(eng, n, b=b, bank=bank, half=half, ks=ks):
                    if half == 0:
                        take(eng, s_t2)
                        pass_on(eng, s_x1_norm_free)
                        if b == batch - 1:
                            pass_on(eng, s_x_res_free)
                        if b == 0:
                            take(eng, s_x1_split_free)
                    eng.copy(x1_hi[:, ks, b * P:(b + 1) * P],
                             wide[bank][:, half * HALF:(half + 1) * HALF].rearrange("p (k t) -> p k t", t=P)
                             ).then_inc(s_x1_hi, 1)
                q.add("scalar", at["t2_high"][b] + half, high)
            for half in range(2):
                ks = slice(half * KD // 2, (half + 1) * KD // 2)

                def low(eng, n, b=b, bank=bank, half=half, ks=ks):
                    if half == 0:
                        take(eng, s_x1_hi, 2)
                    ins = eng.tensor_tensor(
                        x1_lo[:, ks, b * P:(b + 1) * P],
                        wide[bank][:, half * HALF:(half + 1) * HALF].rearrange("p (k t) -> p k t", t=P),
                        x1_hi[:, ks, b * P:(b + 1) * P].bitcast(F32), ALU.subtract)
                    if half == 1:
                        ins.then_inc(s_x1_split, 1)
                q.add("vector", at["t2_high"][b] + 2 + half, low)

        def keep_x1(q, slot):
            def keep(eng, n):
                eng.tensor_scalar(x1[:, :, :].rearrange("p b d -> p (b d)"),
                                  x_res[:, :, :].rearrange("p b d -> p (b d)"), 0.0, 1.0, ALU.add,
                                  ALU.mult).then_inc(s_pool_self, 1)
                take(eng, s_pool_self)
                pass_on(eng, s_x_res_free)
            q.add("gpsimd", slot, keep)

        def tail(q, at, last=False):
            for b in range(batch):
                c = at["z_copy"][b]
                for half in range(2):
                    def rescale(eng, n, b=b, half=half):
                        hs = slice(half * HALF, (half + 1) * HALF)
                        if half == 0 and b == 0:
                            take(eng, s_out_stored, 16)
                        if half == 0:
                            take(eng, s_z_psum)
                            if b == batch - 1:
                                pass_on(eng, s_fused_split_free)
                        eng.tensor_tensor(z[:, b, hs], wide[2 + b][:, hs], down_scale_rows[:, hs],
                                          ALU.mult).then_inc(s_self["z"], 1)
                    q.add("vector", c + half, rescale)

                def free_bank(eng, n, b=b):
                    take(eng, s_self["z"], 2)
                    pass_on(eng, s_wide_free[2 + b])
                q.add("vector", c + 2, free_bank)
                ln_stats(q, at["z_halves"][b], at["z_whole"][b], "z", z, b)

                ln_apply(q, at["z_norm"][b], "z", z, z, b, s_z_norm_self if last and b == batch - 1 else s_z_norm)

                if last and b == batch - 1:
                    for half in range(2):
                        def last_residual(eng, n, b=b, half=half, hs=slice(half * HALF, (half + 1) * HALF)):
                            if half == 0:
                                take(eng, s_z_norm_self, 2)
                            eng.tensor_tensor(z[:, b, hs], z[:, b, hs], x1[:, b, hs], ALU.add).then_inc(
                                s_last_ready, 1)
                        q.add("vector", at["residual"] + half, last_residual)
                    continue

                def residual(eng, n, b=b):
                    take(eng, s_z_norm, 2)
                    ins = eng.tensor_tensor(z[:, b, :], z[:, b, :], x1[:, b, :], ALU.add)
                    if last or b == batch - 1:
                        ins.then_inc(s_pool_self, 1)
                        take(eng, s_pool_self)
                        pass_on(eng, s_out_ready)
                q.add("gpsimd", at["z_norm"][b] + 1, residual)

            def store(eng, n):
                take(eng, s_out_ready)
                if isinstance(n, int):
                    dst = out_blocks[n - 2]
                else:
                    dst = out_blocks[bass.ds(n - 2, 1)].rearrange("o t b d -> (o t) b d")
                eng.dma_start(dst, z[:, :, :]).then_inc(s_out_stored, 16)

            def store_by_time(eng, n):
                for g in range(GROUPS):
                    if g < GROUPS - 1:
                        take(eng, s_out_ready)
                    else:
                        take(eng, s_last_ready, 2)
                    for b in range(batch):
                        eng.dma_start(out_blocks[NB - 1][g * TH:(g + 1) * TH, b, :], z[b * TH:(b + 1) * TH, g, :]
                                      ).then_inc(s_last_stored, 16)
            q.add("sync", at["z_norm"][-1] + 2, store_by_time if last else store)

        AT_BEFORE = {"x_halves": ((4, 5), (8, 9)), "x_whole": (10, 10), "x_norm": (16, 18), "t1": (23, 23),
                     "t1_copy": (25, 26, 27, 28), "u": (43, 50, 58, 66), "u_copy": (51, 59, 64, 74), "pairs": 75}
        AT_REST = {"next_to_last": (0, 2, 3, 5), "last": (4, 6, 7, 8), "down": 24}
        AT_AFTER = {"y": (0, 28), "y_copy": (23, 44), "y_norm": (30, 51), "r": (36, 56), "r_norm": (41, 61),
                    "t2": (57, 65), "t2_high": (57, 66), "keep": 68}
        AT_FFN = 73
        AT_TAIL = {"z_copy": (28, 32), "z_halves": ((34, 35), (38, 39)), "z_whole": (40, 40),
                   "z_norm": (53, 64)}
        START_BEFORE = {"x_halves": ((0, 1), (4, 5)), "x_whole": (2, 6), "x_norm": (7, 9), "t1": (20, 27),
                        "t1_copy": (22, 23, 28, 29), "u": (26, 30), "u_copy": (30, 34), "pieces": 13,
                        "w_in": (0, 4, 8, 12)}
        FIRST_U = {"u": (0, 1), "u_copy": (8, 16)}

        LAST_SCAN_AFTER = {"y": (0, 28), "y_copy": (23, 44), "y_norm": (30, 51), "r": (36, 56), "r_norm": (41, 61),
                      "t2": (57, 64), "t2_high": (57, 65), "keep": 68}
        LAST_SCAN_FFN = 85
        LAST_SCAN_CHUNKS = 9
        BY_TIME_AFTER = {"y": (66, 0), "x_res": 72, "y_copy": (87, 15), "y_norm": (97, 19.9), "r": (104, 23),
                   "r_norm": (110, 27), "t2": (32, 32), "t2_high": (32, 34), "keep": 60}
        NO_SCAN_USE = ((0, 0.3, 0.4, 1), (2, 2.3, 2.4, 3))
        NO_SCAN_FFN = 16
        NO_SCAN_TAIL = {"z_copy": (38, 40), "z_halves": ((46, 47), (48, 49)), "z_whole": (50, 50),
                     "z_norm": (54, 57)}
        BY_TIME_FFN = 39
        BY_TIME_TAIL = {"z_copy": (0, 5), "z_halves": ((2, 3), (8, 9)), "z_whole": (4, 10), "z_norm": (6.5, 12),
                        "residual": 14}

        def period(n, scan, next_block, finished, load_next=None):
            q = Queue()
            last_scan = scan and not next_block
            if n > 0 and n <= NB:
                copy_states(q, 0, SLICES - 1, tell=True, by_time=(n == NB))
            if scan:
                if n > 0:
                    place_u(q, 0, SLICES - 1)
                recurrence(q)
                for s in range(SLICES - 1):
                    copy_states(q, (46, 65 if last_scan else 74, 97)[s], s, tell=last_scan and (s + 1) * TS == TH,
                                by_time=last_scan)
            if finished and scan:
                ffn_rest(q, AT_REST)
                tail(q, AT_TAIL)
            if next_block:
                before(q, AT_BEFORE, load_next)
                for s in range(SLICES - 1):
                    place_u(q, (75, 76, 98)[s], s)
            if n > 0 and next_block:
                for b in range(batch):
                    project_y(q, AT_AFTER["y"][b], b, first=(n == 1))
                load_residual(q)
                for b in range(batch):
                    norms(q, AT_AFTER, b)
                    transpose_and_split(q, AT_AFTER, b)
                keep_x1(q, AT_AFTER["keep"])
                ffn_chunks(q, AT_FFN, 0, CHUNKS_IN_TIME, CHUNKS_IN_TIME - 1, first=(n == 1))
            if last_scan:
                for b in range(batch):
                    project_y(q, LAST_SCAN_AFTER["y"][b], b)
                load_residual(q)
                for b in range(batch):
                    norms(q, LAST_SCAN_AFTER, b)
                    transpose_and_split(q, LAST_SCAN_AFTER, b)
                keep_x1(q, LAST_SCAN_AFTER["keep"])
                ffn_chunks(q, LAST_SCAN_FFN, 0, LAST_SCAN_CHUNKS, LAST_SCAN_CHUNKS - len(NO_SCAN_USE))
                load_last_residual(q, BY_TIME_AFTER["x_res"])
                project_y(q, BY_TIME_AFTER["y"][0], 0, by_time=True)
                norms(q, BY_TIME_AFTER, 0, by_time=True)
            if n == NB:
                project_y(q, BY_TIME_AFTER["y"][1], 1, by_time=True)
                for i, slots in enumerate(NO_SCAN_USE, LAST_SCAN_CHUNKS - len(NO_SCAN_USE)):
                    gate_up_use(q, i, *slots)
                ffn_chunks(q, NO_SCAN_FFN, LAST_SCAN_CHUNKS, KI, KI, beside=False)
                tail(q, NO_SCAN_TAIL)
                norms(q, BY_TIME_AFTER, 1, by_time=True)
                for g in range(GROUPS):
                    transpose_and_split(q, BY_TIME_AFTER, g, by_time=True)
                keep_x1(q, BY_TIME_AFTER["keep"])
                ffn_chunks(q, BY_TIME_FFN, 0, KI, KI, by_time=True, beside=False)
            if n == NB + 1:
                tail(q, BY_TIME_TAIL, last=True)
            return q

        PIECES_START, PIECES_FIRST = 6, 27
        assert PIECES_FIRST >= GATE_UP_PIECES

        start = Queue()
        setup(start)
        before(start, START_BEFORE, lambda n: 1, first=True)
        slots = iter(range(START_BEFORE["pieces"], 1000))
        for i in range(PIECES_START):
            convert(start, i, slots)
        first_period = period(0, True, True, False, lambda n: 2)

        first_u(start, START_BEFORE, 0)
        first_u(first_period, FIRST_U, 1)
        late_loads(first_period, range(20, T, (T - 20) // KH))
        slots = first_period.free_slots("vector", 1, T)
        for i in range(PIECES_START, PIECES_FIRST):
            convert(first_period, i, slots)

        second = period(1, True, True, False, lambda n: n + 2)
        second.add("vector", 0, lambda eng, n: take(eng, s_const_in, 64), rank=-3)
        slots = second.free_slots("vector", 1, T)
        guard_weights(second, slots, 0, GATE_UP_PIECES, up_q[:, KD - 1, inner - 1:inner])
        for i in range(PIECES_FIRST, NP):
            convert(second, i, slots)
        guard_weights(second, slots, GATE_UP_PIECES, NP, down_q[:, KI - 1, dim - 1:dim])
        periods = [(start, 0, 1), (first_period, 0, 1)]

        def last_weights(eng, n):
            for i in range(DOWN_IN_TIME, KI):
                take(eng, s_converted["gpsimd" if by_pool(GATE_UP_PIECES + i) else "vector"])
            take(eng, s_guarded)
        second.add("tensor", T, last_weights)
        periods.append((second, 1, 1))
        periods.append((period(2, True, True, True, lambda n: n + 2), 2, NB - 4))
        periods.append((period(NB - 2, True, True, True), NB - 2, 1))
        periods.append((period(NB - 1, True, False, True), NB - 1, 1))
        periods.append((period(NB, False, False, True), NB, 1))
        periods.append((period(NB + 1, False, False, True), NB + 1, 1))

        def run(name, eng):
            for q, n, turns in periods:
                if turns == 1:
                    q.emit(name, eng, n)
                else:
                    with eng.Fori(n, n + turns) as turn:
                        q.emit(name, eng, turn)

        block = ctx.enter_context(nc.Block())

        @block.sync
        def _(eng):
            for s in s_raw_free + [s_x_res_free, s_x_res_free]:
                eng.sem_inc(s, 1)
            run("sync", eng)
            eng.wait_ge(s_last_stored, 16 * batch * GROUPS)

        @block.tensor
        def _(eng):
            for s in s_wide_free + s_gate_up_free:
                eng.sem_inc(s, 1)
            run("tensor", eng)

        @block.vector
        def _(eng):
            for s, count in ((s_x1_norm_free, batch), (s_fused_free, NF), (s_out_stored, 16)):
                eng.sem_inc(s, count)
            run("vector", eng)

        @block.scalar
        def _(eng):
            for s, count in ((s_x_norm_t_free, 1), (s_u_rows_free, 1), (s_x1_split_free, 1),
                             (s_fused_split_free, NF), (s_slice_copied, SLICES)):
                eng.sem_inc(s, count)
            run("scalar", eng)

        @block.gpsimd
        def _(eng):
            eng.sem_inc(s_states_free, 1)
            run("gpsimd", eng)


def kernel(**inputs):
    import numpy as _np
    import concourse.bacc as _bacc
    from concourse import mybir as _mybir
    from concourse.bass_utils import run_bass_kernel_spmd as _run

    a = {name: _np.asarray(value) for name, value in inputs.items()}

    def columns(v):
        return _np.ascontiguousarray(v.reshape(-1, P).T)

    arrays = {
        "x": a["L0_attn_x"],
        "w_in_t": a["L0_attn_W_in"].T,
        "w_out_t": a["L0_attn_W_out"].T,
        "b_in": columns(a["L0_attn_b_in"]),
        "beta": columns(a["L0_attn_beta"]),
        "gamma": columns(a["L0_attn_gamma"]),
        "b_out": a["L0_attn_b_out"].reshape(1, -1),
        "gate_w": a["L0_ffn_gate_w"],
        "up_w": a["L0_ffn_up_w"],
        "down_w": a["L0_ffn_down_w"],
        "gate_scale": columns(a["L0_ffn_gate_scale"]),
        "up_scale": columns(a["L0_ffn_up_scale"]),
        "down_scale": a["L0_ffn_down_scale"].reshape(1, -1),
        "identity": _np.eye(P, dtype=_np.float32),
    }
    arrays = {name: _np.ascontiguousarray(value) for name, value in arrays.items()}
    nc = _bacc.Bacc("TRN2", target_bir_lowering=False, num_devices=1)
    args = [nc.dram_tensor(name, v.shape, _mybir.dt.from_np(v.dtype), kind="ExternalInput").ap()
            for name, v in arrays.items()]
    shape = a["L0_attn_x"].shape
    args.append(nc.dram_tensor("out", shape, _mybir.dt.float32, kind="ExternalOutput").ap())
    recurrent_sandwich_kernel(nc, *args)
    r = _run(nc, [arrays], core_ids=[0])
    return r.results[0]["out"]
```
